# Optimizing a Trainium2 kernel written in Bass

```python
import numpy as np
import jax
import jax.numpy as jnp

def _softmax(x, axis=-1):
    return jax.nn.softmax(x, axis=axis)

def _gelu(x):
    return jax.nn.gelu(x, approximate=True)

def _silu(x):
    return jax.nn.silu(x)

def _sigmoid(x):
    return jax.nn.sigmoid(x)

def _layernorm(x, axis=-1, eps=1e-05):
    m = jnp.mean(x, axis=axis, keepdims=True)
    v = jnp.var(x, axis=axis, keepdims=True)
    return (x - m) / jnp.sqrt(v + eps)

def _scatter_add(tgt, idx, src, axis=0):
    return tgt.at[idx].add(src)

def _segment_sum(src, seg, n):
    return jax.ops.segment_sum(src, seg, n)
kernel_name = 'mk_recurrent_d1_jaxref_r8_f4af7a'

def setup_inputs(seed: int=0):
    np.random.seed(seed)
    _w = jnp.asarray

    def _L0_attn_setup():
        import jax, jax.numpy as jnp
        import numpy as np
        HIDDEN = 512
        HEAD_DIM = 128
        N_Q_HEADS = 32
        N_KV_HEADS = 8
        SLIDING_WINDOW = 128
        ROPE_THETA = 10000.0
        BATCH, SEQ = (1, 256)

        def _rope(t, pos):
            d = t.shape[-1]
            half = d // 2
            inv_freq = ROPE_THETA ** (-jnp.arange(half, dtype=jnp.float32) / half)
            ang = pos[:, None].astype(jnp.float32) * inv_freq[None, :]
            cos = jnp.cos(ang)[None, :, None, :]
            sin = jnp.sin(ang)[None, :, None, :]
            t1, t2 = (t[..., :half], t[..., half:])
            return jnp.concatenate([t1 * cos - t2 * sin, t1 * sin + t2 * cos], axis=-1)
        key = jax.random.key(seed)
        ks = jax.random.split(key, 5)
        w_scale = HIDDEN ** (-0.5)
        return {'x': jax.random.normal(ks[0], (BATCH, SEQ, HIDDEN), jnp.float32), 'wq': jax.random.normal(ks[1], (HIDDEN, N_Q_HEADS * HEAD_DIM), jnp.float32) * w_scale, 'wk': jax.random.normal(ks[2], (HIDDEN, N_KV_HEADS * HEAD_DIM), jnp.float32) * w_scale, 'wv': jax.random.normal(ks[3], (HIDDEN, N_KV_HEADS * HEAD_DIM), jnp.float32) * w_scale, 'wo': jax.random.normal(ks[4], (N_Q_HEADS * HEAD_DIM, HIDDEN), jnp.float32) * w_scale}
    _L0_attn_in = _L0_attn_setup()

    def _L0_ffn_setup():
        import jax, jax.numpy as jnp
        import numpy as np
        GROUP = 64

        def dequant_q40(w, s, out_features, in_features):
            msb = w >> 4
            lsb = (w & 15 ^ 8) - 8
            g = jnp.concatenate([msb, lsb], axis=1).reshape(-1, GROUP)
            deq = g.astype(s.dtype) * s[:, None]
            return deq.reshape(out_features, in_features)
        key = jax.random.key(seed)
        ks = jax.random.split(key, 7)
        dim, hidden = (512, 1376)
        B, S = (2, 256)

        def packed(k, din, dout):
            return jax.random.randint(k, (din * dout // GROUP // 2, GROUP), -128, 128, dtype=jnp.int32)

        def scales(k, din, dout):
            return (jax.random.uniform(k, (din * dout // GROUP,), dtype=jnp.float32) + 0.5) * 0.01
        x = jax.random.normal(ks[0], (B, S, dim), dtype=jnp.float32)
        w1 = packed(ks[1], dim, hidden)
        s1 = scales(ks[2], dim, hidden)
        w2 = packed(ks[3], hidden, dim)
        s2 = scales(ks[4], hidden, dim)
        w3 = packed(ks[5], dim, hidden)
        s3 = scales(ks[6], dim, hidden)
        return {'x': x, 'w1': w1, 's1': s1, 'w2': w2, 's2': s2, 'w3': w3, 's3': s3}
    _L0_ffn_in = _L0_ffn_setup()
    _d = {'L0_attn_x': _L0_attn_in['x'], 'L0_attn_wq': _L0_attn_in['wq'], 'L0_attn_wk': _L0_attn_in['wk'], 'L0_attn_wv': _L0_attn_in['wv'], 'L0_attn_wo': _L0_attn_in['wo'], 'L0_ffn_w1': _L0_ffn_in['w1'], 'L0_ffn_s1': _L0_ffn_in['s1'], 'L0_ffn_w2': _L0_ffn_in['w2'], 'L0_ffn_s2': _L0_ffn_in['s2'], 'L0_ffn_w3': _L0_ffn_in['w3'], 'L0_ffn_s3': _L0_ffn_in['s3']}
    _x0 = _d['L0_attn_x']
    _d['L0_attn_x'] = jax.random.normal(jax.random.fold_in(jax.random.key(seed), 1), (4, 256, 512), dtype=_x0.dtype)
    del _x0
    return _d

def reference(L0_attn_x, L0_attn_wq, L0_attn_wk, L0_attn_wv, L0_attn_wo, L0_ffn_w1, L0_ffn_s1, L0_ffn_w2, L0_ffn_s2, L0_ffn_w3, L0_ffn_s3):

    def _L0_attn_ref(x, wq, wk, wv, wo):
        import jax, jax.numpy as jnp
        import numpy as np
        HIDDEN = 512
        HEAD_DIM = 128
        N_Q_HEADS = 32
        N_KV_HEADS = 8
        SLIDING_WINDOW = 128
        ROPE_THETA = 10000.0
        BATCH, SEQ = (1, 256)

        def _rope(t, pos):
            d = t.shape[-1]
            half = d // 2
            inv_freq = ROPE_THETA ** (-jnp.arange(half, dtype=jnp.float32) / half)
            ang = pos[:, None].astype(jnp.float32) * inv_freq[None, :]
            cos = jnp.cos(ang)[None, :, None, :]
            sin = jnp.sin(ang)[None, :, None, :]
            t1, t2 = (t[..., :half], t[..., half:])
            return jnp.concatenate([t1 * cos - t2 * sin, t1 * sin + t2 * cos], axis=-1)
        B, S, _ = x.shape
        G = N_Q_HEADS // N_KV_HEADS
        sm_scale = HEAD_DIM ** (-0.5)
        q = (x @ wq).reshape(B, S, N_Q_HEADS, HEAD_DIM)
        k = (x @ wk).reshape(B, S, N_KV_HEADS, HEAD_DIM)
        v = (x @ wv).reshape(B, S, N_KV_HEADS, HEAD_DIM)
        pos = jnp.arange(S)
        q = _rope(q, pos)
        k = _rope(k, pos)
        qg = q.reshape(B, S, N_KV_HEADS, G, HEAD_DIM)
        scores = jnp.einsum('bqhgd,bshd->bhgqs', qg, k) * sm_scale
        i = pos[:, None]
        j = pos[None, :]
        allowed = (j <= i) & (j > i - SLIDING_WINDOW)
        neg = jnp.finfo(scores.dtype).min
        scores = jnp.where(allowed[None, None, None], scores, neg)
        attn = jax.nn.softmax(scores, axis=-1)
        out = jnp.einsum('bhgqs,bshd->bqhgd', attn, v).reshape(B, S, N_Q_HEADS * HEAD_DIM)
        return out @ wo

    def _L0_ffn_ref(x, w1, s1, w2, s2, w3, s3):
        import jax, jax.numpy as jnp
        import numpy as np
        GROUP = 64

        def dequant_q40(w, s, out_features, in_features):
            msb = w >> 4
            lsb = (w & 15 ^ 8) - 8
            g = jnp.concatenate([msb, lsb], axis=1).reshape(-1, GROUP)
            deq = g.astype(s.dtype) * s[:, None]
            return deq.reshape(out_features, in_features)
        dim = x.shape[-1]
        hidden = w1.shape[0] * w1.shape[1] * 2 // dim
        W1 = dequant_q40(w1, s1, hidden, dim)
        W3 = dequant_q40(w3, s3, hidden, dim)
        W2 = dequant_q40(w2, s2, dim, hidden)
        a = jnp.einsum('bsd,hd->bsh', x, W1)
        b = jnp.einsum('bsd,hd->bsh', x, W3)
        h = jax.nn.silu(a) * b
        return jnp.einsum('bsh,dh->bsd', h, W2)
    x = L0_attn_x
    xn = _layernorm(x, axis=-1)
    s = _L0_attn_ref(xn, L0_attn_wq, L0_attn_wk, L0_attn_wv, L0_attn_wo)
    g = _silu(_L0_ffn_ref(xn, L0_ffn_w1, L0_ffn_s1, L0_ffn_w2, L0_ffn_s2, L0_ffn_w3, L0_ffn_s3))
    x = x + s * g
    return x

_drawn_inputs = setup_inputs


def setup_inputs(seed=0):
    import zlib

    import numpy as np

    out = dict(_drawn_inputs(seed))
    spreads = {}
    factors = {}
    for name, (base, spread) in spreads.items():
        noise = np.random.default_rng([zlib.crc32(name.encode()), seed]).standard_normal(out[name].shape)
        drawn = base * np.exp(spread * noise) if base else spread * noise
        out[name] = jnp.asarray(drawn.astype(out[name].dtype))
    for name, factor in factors.items():
        out[name] = (out[name] * factor).astype(out[name].dtype)
    return out
```

```python
from contextlib import ExitStack

import numpy as np
import concourse.bass as bass
from concourse import mybir

B, SEQ, D = 4, 256, 512
HD, NQ, NKV = 128, 32, 8
GH = NQ // NKV
HALF = HD // 2
F = 1376
GROUP = 64
P = 128
TOK = B * SEQ
NT = TOK // P
DT = D // P
IT = 512
FT = -(-F // P)
FR = F - (FT - 1) * P
PK = D // 2
R2 = F * D // 2 // GROUP // P
EPS = 1e-5
SM = float(HD) ** -0.5
NEG = -3.0e38
RING = 5
CHUNKS = 6 + GH
ALL_W = CHUNKS * NKV
C_COS, C_SIN, C_MASK, C_ID, C_W = 0, SEQ, 2 * SEQ, 2 * SEQ + 3 * P, 2 * SEQ + 4 * P


def build(nc, x, wq, wk, wv, wo, w1, s1, w2, s2, w3, s3, const, out):
    f32, f32r, i32 = mybir.dt.float32, mybir.dt.float32r, mybir.dt.int32
    ALU, ACT = mybir.AluOpType, mybir.ActivationFunctionType

    x_v = x.rearrange("b (t p) d -> p (b t) d", p=P)
    out_v = out.rearrange("b (t p) d -> p (b t) d", p=P)
    wq_v = wq.rearrange("(t p) n -> p t n", p=P)
    wk_v = wk.rearrange("(t p) n -> p t n", p=P)
    wv_v = wv.rearrange("(t p) n -> p t n", p=P)
    w13_v = [w.rearrange("(h r) c -> h (r c)", r=PK // GROUP) for w in (w1, w3)]
    s13_v = [s.rearrange("(h g) -> h g", g=D // GROUP) for s in (s1, s3)]
    w2_v = w2.rearrange("(p r) c -> p (r c)", r=R2)
    s2_v = s2.rearrange("(p g) -> p g", g=2 * R2)

    ctx = ExitStack()
    with ctx:
        def sb(name, shape, dt, at=ctx):
            return at.enter_context(nc.sbuf_tensor(name, shape, dt))

        def sem(name):
            return ctx.enter_context(nc.semaphore(name))

        gate = sb("gate", [P, NT, D], f32)
        cst = sb("cst", [P, C_W], f32)
        cos, sin = cst[:, C_COS:C_COS + SEQ], cst[:, C_SIN:C_SIN + SEQ]
        mask, ident = cst[:, C_MASK:C_MASK + 3 * P], cst[:, C_ID:C_ID + P]
        raw = sb("raw", [P, RING, D], f32)
        xh = sb("xh", [P, DT, TOK], f32r)
        xl = sb("xl", [P, DT, TOK], f32r)
        main = ctx.enter_context(ExitStack())

        ffn = ctx.enter_context(ExitStack())
        packed = sb("packed", [P, 4, 2, PK], i32, ffn)
        s13 = sb("s13", [P, FT, 2, D // GROUP], f32, ffn)
        nib = sb("nib", [P, 2, 2 * PK], i32, ffn)
        W13 = sb("W13", [P, 2, 2, D], f32, ffn)
        W13h = sb("W13h", [P, 2, 2, DT, P], f32r, ffn)
        W13l = sb("W13l", [P, 2, 2, DT, P], f32r, ffn)
        act_h = sb("act_h", [P, 2, IT], f32, ffn)
        NR2 = 11
        packed2 = sb("packed2", [P, 2, NR2 * GROUP], i32, ffn)
        nib2 = sb("nib2", [P, 2, NR2 * GROUP], i32, ffn)
        s2s = sb("s2s", [P, 2 * R2], f32, ffn)
        W2h = sb("W2h", [P, FT, D], f32r, ffn)
        W2l = sb("W2l", [P, FT, D], f32r, ffn)
        stat = sb("stat", [P, NT, 6], f32, ffn)
        mv = sb("mv", [P, NT, 2], f32, ffn)
        std = sb("std", [P, 4, NT], f32, ffn)
        early = ffn.enter_context(ExitStack())
        xn = sb("xn", [P, NT, D], f32, early)
        W2n = sb("W2n", [P, R2, 2, GROUP], f32, early)
        early.close()
        hid_hl = sb("hid_hl", [P, 2, 2, 2, TOK], f32r, ffn)
        hh = [hid_hl[:, s // 2, 0, s % 2, :] for s in range(4)]
        hl = [hid_hl[:, s // 2, 1, s % 2, :] for s in range(4)]
        ffn.close()

        wih = sb("wih", [P, 6, DT, P], f32r, main)
        wil = sb("wil", [P, 6, DT, P], f32r, main)
        woh = sb("woh", [P, GH, D], f32r, main)
        wol = sb("wol", [P, GH, D], f32r, main)
        q = sb("q", [P, 2, GH, IT], f32, main)
        k = sb("k", [P, 2, IT], f32, main)
        vT = sb("vT", [P, IT], f32, main)
        vh = sb("vh", [P, 2, IT // P, HD], f32r, main)
        vl = sb("vl", [P, 2, IT // P, HD], f32r, main)
        swap = sb("swap", [P, 2, IT], f32, main)
        probs = sb("probs", [P, 2 * GH, 3 * P], f32, main)
        mx = sb("mx", [P, 2 * GH, 2], f32, main)
        pace = sb("pace", [P, 2], f32, main)
        nmx = sb("nmx", [P, 2 * GH, 2], f32, main)
        rsum = sb("rsum", [P, 2 * GH, 2], f32, main)
        rinv = sb("rinv", [P, 2 * GH, 2], f32, main)
        ph = sb("ph", [P, 3, GH * P], f32r, main)
        pl = sb("pl", [P, 3, GH * P], f32r, main)
        oh = sb("oh", [P, 4, GH, P], f32r, main)
        ol = sb("ol", [P, 4, GH, P], f32r, main)
        acc = sb("acc", [P, NT, D], f32, main)

        bank = [ctx.enter_context(nc.psum_tensor(f"bank{i}", [P, 512], f32)) for i in range(8)]
        S_B, PJ_B, T_B, O_B = bank[0:2], bank[2:4], bank[4:6], bank[6:8]

        const_in, s13_in, s2_in, out_done = sem("const_in"), sem("s13_in"), sem("s2_in"), sem("out_done")
        x_in = [sem(f"x_in{i}") for i in range(4)]
        w13_in = [sem(f"w13_in{i}") for i in range(4)]
        w2_in = [sem(f"w2_in{i}") for i in range(2)]
        raw_in = [sem(f"raw_in{i}") for i in range(RING)]
        zeroed, stats_done, mv_done, ln_small, std_done = (
            sem("zeroed"), sem("stats_done"), sem("mv_done"), sem("ln_small"), sem("std_done"))
        xn_done, xT_ps, xh_done, xl_done = sem("xn_done"), sem("xT_ps"), sem("xh_done"), sem("xl_done")
        nib_done, W13_done, W13_ps, W13h_done, W13l_done = (
            sem("nib_done"), sem("W13_done"), sem("W13_ps"), sem("W13h_done"), sem("W13l_done"))
        nib2_done, W2_done, W2_ps, W2h_done = sem("nib2_done"), sem("W2_done"), sem("W2_ps"), sem("W2h_done")
        ab_ps, silu_done, h_done, hh_done, hl_done = (
            sem("ab_ps"), sem("silu_done"), sem("h_done"), sem("hh_done"), sem("hl_done"))
        ffn_ps, ffn_read, gate_done = sem("ffn_ps"), sem("ffn_read"), sem("gate_done")
        scores_ps, masked, nmax_done, exp_done, rinv_done, probs_done = (
            sem("scores_ps"), sem("masked"), sem("nmax_done"), sem("exp_done"), sem("rinv_done"),
            sem("probs_done"))
        proj_ps, cos_done, swapped, sin_done, rope_done = (
            sem("proj_ps"), sem("cos_done"), sem("swapped"), sem("sin_done"), sem("rope_done"))
        vT_done, v_ps, vh_done, vl_done = sem("vT_done"), sem("v_ps"), sem("vh_done"), sem("vl_done")
        pT_ps, ph_done, pl_done = sem("pT_ps"), sem("ph_done"), sem("pl_done")
        o_ps, oh_done, ol_done = sem("o_ps"), sem("oh_done"), sem("ol_done")
        y_ps, acc_done = sem("y_ps"), sem("acc_done")
        wh_done, wl_done = sem("wh_done"), sem("wl_done")
        gated, final = sem("gated"), sem("final")

        def wait(eng, s, value):
            if isinstance(value, int) and value <= 0:
                return
            eng.wait_ge(s, value)

        def cnt(per, g, bp, c):
            return 2 * per * g + (per * bp + c)

        def spread(ap, *sizes):
            return ap.to_broadcast(list(sizes))

        block = ctx.enter_context(nc.Block())

        def wo_chunk(g, h):
            return CHUNKS * g + (6 + h)

        def in_chunk(g, c):
            return CHUNKS * g + c

        @block.sync
        def _(sp):
            for i in range(4):
                sp.dma_start(xn[:, 2 * i:2 * i + 2, :], x_v[:, 2 * i:2 * i + 2, :]).then_inc(x_in[i], 16)
                if i == 0:
                    sp.dma_start(cst[:, :], const).then_inc(const_in, 16)

            def load13(t):
                rows = P if t < FT - 1 else FR
                wait(sp, nib_done, t - 3)
                for m in range(2):
                    sp.dma_start(packed[0:rows, t % 4, m, :], w13_v[m][t * P:t * P + rows, :]) \
                        .then_inc(w13_in[t % 4], 16)

            sp.wait_ge(zeroed, 3)
            for m in range(2):
                sp.dma_start(s13[:, 0:FT - 1, m, :],
                             s13_v[m][0:(FT - 1) * P, :].rearrange("(t p) g -> p t g", p=P)).then_inc(s13_in, 16)
                sp.dma_start(s13[0:FR, FT - 1, m, :], s13_v[m][(FT - 1) * P:F, :]).then_inc(s13_in, 16)
            load13(0)
            load13(1)
            sp.dma_start(s2s[:, :], s2_v).then_inc(s2_in, 16)
            for i in range(4):
                r0, r1 = NR2 * i, min(NR2 * i + NR2, R2)
                wait(sp, nib2_done, i - 1)
                sp.dma_start(packed2[:, i % 2, 0:(r1 - r0) * GROUP],
                             w2_v[:, r0 * GROUP:r1 * GROUP]).then_inc(w2_in[i % 2], 16)
                if i < 2:
                    load13(2 + i)
            for t in range(4, FT):
                load13(t)

            def load_in(w, g, c):
                src = (wk_v, wv_v)[c][:, :, bass.ds(g * HD, HD)] if c < 2 else \
                    wq_v[:, :, bass.ds(g * (GH * HD) + (c - 2) * HD, HD)]
                s = w if isinstance(w, int) else c + CHUNKS
                sp.dma_start(raw[:, s % RING, :].rearrange("p (t n) -> p t n", t=DT), src) \
                    .then_inc(raw_in[s % RING], 16)

            for c in range(6):
                wait(sp, wl_done, c - RING + 1)
                load_in(c, 0, c)

            def group_loads(g, last):
                for h in range(GH):
                    wait(sp, wl_done, wo_chunk(g, h) - RING + 1)
                    sp.dma_start(raw[:, (6 + h) % RING, :], wo[bass.ds(g * (GH * HD) + h * HD, HD), :]) \
                        .then_inc(raw_in[(6 + h) % RING], 16)
                if not last:
                    for c in range(6):
                        wait(sp, wl_done, in_chunk(g + 1, c) - RING + 1)
                        load_in(None, g + 1, c)

            group_loads(0, False)
            with sp.Fori(1, NKV - 1) as g:
                group_loads(g, False)
            group_loads(NKV - 1, True)
            for t in range(NT + RING):
                if t < NT:
                    if t < RING:
                        sp.wait_ge(wl_done, ALL_W + t - RING + 1)
                    else:
                        sp.wait_ge(final, t - RING + 1)
                    sp.dma_start(raw[:, (ALL_W + t) % RING, :], x_v[:, t, :]).then_inc(raw_in[(ALL_W + t) % RING], 16)
                if t >= RING:
                    sp.wait_ge(final, t - RING + 1)
                    sp.dma_start(out_v[:, t - RING, :], gate[:, t - RING, :]).then_inc(out_done, 16)
            sp.wait_ge(out_done, 16 * NT)

        @block.gpsimd
        def _(pool):
            def hid_lo(t, s4):
                for half in range(2):
                    pool.wait_ge(hh_done, 2 * t + (half + 1))
                    cols = slice(half * IT, half * IT + IT)
                    nc.gpsimd.tensor_tensor(hl[s4][:, cols], act_h[:, half, :], hh[s4][:, cols].bitcast(f32),
                                            ALU.subtract).then_inc(hl_done, 1)

            for t in range(2):
                hid_lo(t, t)
            with pool.Fori(0, 2) as v:
                for j in range(4):
                    hid_lo(4 * v + (2 + j), (2 + j) % 4)
            hid_lo(FT - 1, (FT - 1) % 4)

            def w_lo(w, slot, hi, lo):
                pool.wait_ge(wh_done, w + 1)
                nc.gpsimd.tensor_tensor(lo, raw[:, slot, :], hi.bitcast(f32), ALU.subtract).then_inc(wl_done, 1)

            def flat(ap):
                return ap.rearrange("p t n -> p (t n)")

            def lo_in(g, c):
                w_lo(in_chunk(g, c), c % RING, flat(wih[:, c]), flat(wil[:, c]))

            def lo_wo(g, h):
                w_lo(wo_chunk(g, h), (6 + h) % RING, woh[:, h, :], wol[:, h, :])

            def sin_part(g, bp, c):
                s = (5 * bp + c) % 2
                pool.wait_ge(swapped, cnt(5, g, bp, c + 1))
                v = swap[:, s, :].rearrange("p (b n) -> p b n", b=2)
                nc.gpsimd.tensor_tensor(v, v, spread(sin.unsqueeze(1), P, 2, SEQ), ALU.mult).then_inc(sin_done, 1)

            pool.wait_ge(gate_done, 1)
            for c in range(6):
                lo_in(0, c)
            for c in range(5):
                sin_part(0, 0, c)

            def step(g, bp, last):
                ng, nbp = (g, 1) if bp == 0 else (g + 1, 0)
                more = not (last and bp == 1)
                w = bp == 0
                nxt = w and not last
                if more:
                    sin_part(ng, nbp, 0)
                if w:
                    lo_wo(g, 0)
                    lo_wo(g, 1)
                    lo_wo(g, 2)
                    lo_wo(g, 3)
                if more:
                    sin_part(ng, nbp, 1)
                if nxt:
                    lo_in(g + 1, 0)
                if more:
                    sin_part(ng, nbp, 2)
                if nxt:
                    lo_in(g + 1, 1)
                if more:
                    sin_part(ng, nbp, 3)
                if nxt:
                    lo_in(g + 1, 2)
                if more:
                    sin_part(ng, nbp, 4)
                if nxt:
                    lo_in(g + 1, 3)
                    lo_in(g + 1, 4)
                    lo_in(g + 1, 5)

            def group(g, last=False):
                step(g, 0, last)
                step(g, 1, last)

            group(0)
            with pool.Fori(1, NKV - 1) as g:
                group(g)
            group(NKV - 1, True)

        @block.scalar
        def _(act):
            act.wait_ge(ln_small, 1)
            nc.scalar.activation(std[:, 1, :], std[:, 0, :], ACT.Sqrt).then_inc(std_done, 1)
            for i in range(NT):
                act.wait_ge(xT_ps, i + 1)
                nc.scalar.activation(xh[:, :, i * P:(i + 1) * P],
                                     bank[i % 4][:, :].rearrange("p (t n) -> p t n", t=DT),
                                     ACT.Copy).then_inc(xh_done, 1)

            def w13_hi(t, s2_):
                for m in range(2):
                    act.wait_ge(W13_ps, 2 * t + (m + 1))
                    wait(act, ab_ps, 4 * t - 4)
                    nc.scalar.activation(W13h[:, s2_, m].rearrange("p t n -> p (t n)"), bank[m][:, :],
                                         ACT.Copy).then_inc(W13h_done, 1)

            def hidden(t, u, s4):
                for half in range(2):
                    act.wait_ge(ab_ps, 4 * t + (2 * half + 1))
                    wait(act, hl_done, 2 * t + (half - 1))
                    nc.scalar.activation(act_h[:, half, :], bank[2 + 2 * half][:, :], ACT.Silu) \
                        .then_inc(silu_done, 1)
                for half in range(2):
                    act.wait_ge(h_done, 2 * t + (half + 1))
                    if not isinstance(u, int) or u:
                        act.wait_ge(ffn_read, 8 * u + (FT - 8))
                    nc.scalar.activation(hh[s4][:, half * IT:half * IT + IT], act_h[:, half, :],
                                         ACT.Copy).then_inc(hh_done, 1)

            def w2_hi(t):
                act.wait_ge(W2_ps, t + 1)
                nc.scalar.activation(W2h[:, t, :].rearrange("h (p j) -> h j p", j=4)[0:(P if t < FT - 1 else FR)],
                                     bank[6 + t % 2][0:(P if t < FT - 1 else FR), :]
                                     .rearrange("h (j p) -> h j p", j=4), ACT.Copy).then_inc(W2h_done, 1)

            w13_hi(0, 0)
            w13_hi(1, 1)
            hidden(0, 0, 0)
            for t in range(6):
                w2_hi(t)
            w13_hi(2, 0)
            hidden(1, 0, 1)
            for t in range(6, FT):
                w2_hi(t)
            with act.Fori(0, 2) as v:
                for j in range(4):
                    w13_hi(4 * v + (3 + j), (3 + j) % 2)
                    hidden(4 * v + (2 + j), 2 * v + (1 + j // 2), (2 + j) % 4)
            hidden(FT - 1, FT // 2, (FT - 1) % 4)
            act.wait_ge(ffn_read, FT + 6 * NT)
            for i in range(2):
                nc.scalar.activation(gate[:, 4 * i:4 * i + 4, :], gate[:, 4 * i:4 * i + 4, :], ACT.Silu) \
                    .then_inc(gate_done, 1)

            def w_hi(slot, use, hi):
                act.wait_ge(raw_in[slot], 16 * use)
                nc.scalar.activation(hi, raw[:, slot, :], ACT.Copy).then_inc(wh_done, 1)

            def hi_in(g, c):
                wait(act, proj_ps, cnt(6, g, -1, c + 1))
                w_hi(c % RING, 2 * g + (c // RING + 1), wih[:, c].rearrange("p t n -> p (t n)"))

            def hi_wo(g, h):
                wait(act, y_ps, 8 * g)
                w_hi((6 + h) % RING, 2 * g + ((6 + h) // RING + 1), woh[:, h, :])

            def halves(g, bp, c):
                a = 5 * bp + c
                act.wait_ge(proj_ps, cnt(6, g, bp, (c + 2 if c else 1)))
                wait(act, rope_done, cnt(5, g, bp, c - 1))
                src = PJ_B[(c + 1 if c else 0) % 2]
                nc.scalar.activation(swap[0:HALF, a % 2, :], src[HALF:P, :], ACT.Copy)
                nc.scalar.activation(swap[HALF:P, a % 2, :], src[0:HALF, :], ACT.Copy).then_inc(swapped, 1)

            def v_out(g, bp):
                act.wait_ge(proj_ps, cnt(6, g, bp, 2))
                wait(act, v_ps, cnt(1, g, bp, 0))
                nc.scalar.activation(vT[:, :], PJ_B[1][:, :], ACT.Copy).then_inc(vT_done, 1)

            def v_hi(g, bp, t_bank):
                act.wait_ge(v_ps, cnt(1, g, bp, 1))
                wait(act, o_ps, cnt(4, g, bp, -4))
                nc.scalar.activation(vh[:, bp].rearrange("p t n -> p (t n)"), t_bank[:, :],
                                     ACT.Copy).then_inc(vh_done, 1)

            def exps(g, bp, b, h):
                s = 4 * b + h
                act.wait_ge(nmax_done, cnt(8, g, bp, s + 1))
                for i, (c0, c1) in enumerate(((0, P), (P, 3 * P))):
                    e = nc.scalar.activation(probs[:, s, c0:c1], probs[:, s, c0:c1], ACT.Exp,
                                             bias=nmx[:, s, i:i + 1], scale=SM, accum_out=rsum[:, s, i:i + 1])
                e.then_inc(exp_done, 1)

            def p_hi(g, bp, b, r):
                j = 4 * b + r
                act.wait_ge(pT_ps, cnt(6, g, bp, 3 * b + r + 1))
                wait(act, o_ps, cnt(4, g, bp, 2 * b))
                nc.scalar.activation(ph[:, r, :], T_B[(7 * bp + j) % 2][:, :], ACT.Copy).then_inc(ph_done, 1)

            def o_hi(g, bp, j):
                act.wait_ge(o_ps, cnt(4, g, bp, j + 1))
                wait(act, y_ps, cnt(4, g, bp, j - 3))
                nc.scalar.activation(oh[:, j].rearrange("p h n -> p (h n)"), O_B[j % 2][:, :],
                                     ACT.Copy).then_inc(oh_done, 1)

            for c in range(6):
                hi_in(0, c)
            halves(0, 0, 0)
            v_out(0, 0)
            halves(0, 0, 1)
            v_hi(0, 0, T_B[1])
            for c in range(2, 5):
                halves(0, 0, c)
            for h in range(GH):
                exps(0, 0, 0, h)

            def step(g, bp, last):
                ng, nbp = (g, 1) if bp == 0 else (g + 1, 0)
                more = not (last and bp == 1)
                w = bp == 0
                nxt = w and not last
                for r in range(3):
                    p_hi(g, bp, 0, r)
                if more:
                    halves(ng, nbp, 0)
                    v_out(ng, nbp)
                if w:
                    hi_wo(g, 0)
                    hi_wo(g, 1)
                o_hi(g, bp, 0)
                o_hi(g, bp, 1)
                if w:
                    hi_wo(g, 2)
                    hi_wo(g, 3)
                for h in range(GH):
                    exps(g, bp, 1, h)
                if more:
                    halves(ng, nbp, 1)
                    v_hi(ng, nbp, T_B[(7 * bp + 3) % 2])
                if nxt:
                    hi_in(g + 1, 0)
                if more:
                    halves(ng, nbp, 2)
                if nxt:
                    hi_in(g + 1, 1)
                if more:
                    halves(ng, nbp, 3)
                for r in range(3):
                    p_hi(g, bp, 1, r)
                if nxt:
                    hi_in(g + 1, 2)
                if more:
                    halves(ng, nbp, 4)
                o_hi(g, bp, 2)
                o_hi(g, bp, 3)
                if nxt:
                    hi_in(g + 1, 3)
                if more:
                    for h in range(GH):
                        exps(ng, nbp, 0, h)
                if nxt:
                    hi_in(g + 1, 4)
                    hi_in(g + 1, 5)

            def group(g, last=False):
                step(g, 0, last)
                step(g, 1, last)

            group(0)
            with act.Fori(1, NKV - 1) as g:
                group(g)
            group(NKV - 1, True)

        @block.vector
        def _(dve):
            nc.vector.memset(gate[:, :, :], 0.0).then_inc(zeroed, 1)
            nc.vector.memset(s13[:, FT - 1, :, :], 0.0).then_inc(zeroed, 1)
            nc.vector.memset(packed[:, (FT - 1) % 4, :, :], 0).then_inc(zeroed, 1)
            nc.vector.memset(W2h[FR:P, FT - 1, :].bitcast(f32), 0.0).then_inc(zeroed, 1)
            nc.vector.memset(W2l[FR:P, FT - 1, :].bitcast(f32), 0.0).then_inc(zeroed, 1)

            for i in range(NT):
                dve.wait_ge(x_in[i // 2], 16)
                nc.vector.bn_stats(stat[:, i, :], xn[:, i, :]).then_inc(stats_done, 1)
            for i in range(NT):
                dve.wait_ge(stats_done, i + 1)
                nc.vector.bn_aggr(mv[:, i, :], stat[:, i, :]).then_inc(mv_done, 1)
            dve.wait_ge(mv_done, NT)
            nc.vector.tensor_scalar(std[:, 0, :], mv[:, :, 1], EPS, None, ALU.add).then_inc(ln_small, 1)
            dve.wait_ge(std_done, 1)
            nc.vector.reciprocal(std[:, 2, :], std[:, 1, :]).then_inc(ln_small, 1)
            dve.wait_ge(ln_small, 2)
            nc.vector.tensor_tensor(std[:, 3, :], std[:, 2, :], std[:, 2, :], ALU.mult).then_inc(ln_small, 1)
            dve.wait_ge(ln_small, 3)
            nc.vector.tensor_tensor(std[:, 1, :], std[:, 3, :], std[:, 0, :], ALU.mult).then_inc(ln_small, 1)
            dve.wait_ge(ln_small, 4)
            nc.vector.tensor_scalar(std[:, 3, :], std[:, 1, :], -0.5, 1.5, ALU.mult, ALU.add).then_inc(ln_small, 1)
            dve.wait_ge(ln_small, 5)
            nc.vector.tensor_tensor(std[:, 1, :], std[:, 3, :], std[:, 2, :], ALU.mult).then_inc(ln_small, 1)
            dve.wait_ge(ln_small, 6)
            for i in range(NT):
                nc.vector.tensor_scalar(xn[:, i, :], xn[:, i, :], mv[:, i, 0:1], std[:, 1, i:i + 1],
                                        ALU.subtract, ALU.mult).then_inc(xn_done, 1)

            def x_lo(i):
                dve.wait_ge(xh_done, i + 1)
                cols = slice(i * P, (i + 1) * P)
                nc.vector.tensor_tensor(xl[:, :, cols], bank[i % 4][:, :].rearrange("p (t n) -> p t n", t=DT),
                                        xh[:, :, cols].bitcast(f32), ALU.subtract).then_inc(xl_done, 1)

            def dequant13(t, s4, use):
                dve.wait_ge(w13_in[s4], 32 * use)
                wait(dve, W13_done, t)
                src = packed[:, s4].rearrange("p m c -> p (m c)")
                nc.vector.tensor_scalar(nib[:, 0, :], src, 4, None, ALU.arith_shift_right)
                nc.vector.tensor_scalar(nib[:, 1, :], src, 15, 8, ALU.bitwise_and, ALU.bitwise_xor) \
                    .then_inc(nib_done, 1)
                dve.wait_ge(nib_done, t + 1)
                wait(dve, W13_ps, 2 * t - 2)
                n = [nib[:, i, :].rearrange("p (g c) -> p g c", c=GROUP) for i in range(2)]
                sc = s13[:, bass.ds(t, 1), :, :].rearrange("p o m (g n) -> p n (o m g)", n=2)
                o = W13[:, s4 % 2].rearrange("p m (g n c) -> p n (m g) c", n=2, c=GROUP)
                GS = 2 * DT
                nc.vector.tensor_tensor(o[:, 0], n[0], spread(sc[:, 0].unsqueeze(2), P, GS, GROUP), ALU.mult)
                nc.vector.scalar_tensor_tensor(out=o[:, 1], in0=n[1], scalar=-8.0,
                                               in1=spread(sc[:, 1].unsqueeze(2), P, GS, GROUP),
                                               op0=ALU.add, op1=ALU.mult).then_inc(W13_done, 1)

            def w13_lo(t, s2_):
                for m in range(2):
                    dve.wait_ge(W13h_done, 2 * t + (m + 1))
                    nc.vector.tensor_tensor(W13l[:, s2_, m].rearrange("p t n -> p (t n)"), bank[m][:, :],
                                            W13h[:, s2_, m].rearrange("p t n -> p (t n)").bitcast(f32),
                                            ALU.subtract).then_inc(W13l_done, 1)

            def hid(t):
                for half in range(2):
                    dve.wait_ge(silu_done, 2 * t + (half + 1))
                    dve.wait_ge(ab_ps, 4 * t + (2 * half + 2))
                    nc.vector.tensor_tensor(act_h[:, half, :], act_h[:, half, :], bank[3 + 2 * half][:, :],
                                            ALU.mult).then_inc(h_done, 1)

            def dequant2(i):
                r0, r1 = NR2 * i, min(NR2 * i + NR2, R2)
                n = r1 - r0
                dve.wait_ge(w2_in[i % 2], 16 * (i // 2 + 1))
                wait(dve, W2_done, i)
                src = packed2[:, i % 2, 0:n * GROUP]
                nc.vector.tensor_scalar(nib2[:, 0, 0:n * GROUP], src, 4, None, ALU.arith_shift_right)
                nc.vector.tensor_scalar(nib2[:, 1, 0:n * GROUP], src, 15, 8, ALU.bitwise_and,
                                        ALU.bitwise_xor).then_inc(nib2_done, 1)
                dve.wait_ge(nib2_done, i + 1)
                nb = [nib2[:, a, 0:n * GROUP].rearrange("p (r c) -> p r c", c=GROUP) for a in range(2)]
                sc = s2s[:, 2 * r0:2 * r1].rearrange("p (r n) -> p n r", n=2)
                nc.vector.tensor_tensor(W2n[:, r0:r1, 0, :], nb[0], spread(sc[:, 0].unsqueeze(2), P, n, GROUP),
                                        ALU.mult)
                nc.vector.scalar_tensor_tensor(out=W2n[:, r0:r1, 1, :], in0=nb[1], scalar=-8.0,
                                               in1=spread(sc[:, 1].unsqueeze(2), P, n, GROUP),
                                               op0=ALU.add, op1=ALU.mult).then_inc(W2_done, 1)

            def w2_lo(t):
                rows = P if t < FT - 1 else FR
                dve.wait_ge(W2h_done, t + 1)
                perm = "h (p j) -> h j p"
                nc.vector.tensor_tensor(W2l[:, t, :].rearrange(perm, j=4)[0:rows],
                                        bank[6 + t % 2][0:rows, :].rearrange("h (j p) -> h j p", j=4),
                                        W2h[:, t, :].bitcast(f32).rearrange(perm, j=4)[0:rows],
                                        ALU.subtract).then_inc(ffn_read, 1)

            def ffn_add(u):
                for i in range(NT):
                    dve.wait_ge(ffn_ps, 8 * u + (i + 1))
                    wait(dve, ffn_read, 8 * u + (FT + i - 7))
                    nc.vector.tensor_tensor(gate[:, i, :], gate[:, i, :], bank[6 + (FT + i) % 2][:, :],
                                            ALU.add).then_inc(ffn_read, 1)

            dve.wait_ge(s13_in, 64)
            dve.wait_ge(zeroed, 5)
            dequant13(0, 0, 1)
            for i in range(4):
                x_lo(i)
            dequant13(1, 1, 1)
            for i in range(4, NT):
                x_lo(i)
            w13_lo(0, 0)
            w13_lo(1, 1)
            dve.wait_ge(s2_in, 16)
            for i in range(4):
                dequant2(i)
            hid(0)
            dequant13(2, 2, 1)
            for t in range(6):
                w2_lo(t)
            w13_lo(2, 0)
            hid(1)
            dequant13(3, 3, 1)
            for t in range(6, FT):
                w2_lo(t)
            for t in range(2, FT - 1):
                w13_lo(t + 1, (t + 1) % 2)
                if t + 2 < FT:
                    dequant13(t + 2, (t + 2) % 4, (t + 2) // 4 + 1)
                hid(t)
                if t % 2:
                    ffn_add(t // 2 - 1)
            hid(FT - 1)
            ffn_add(FT // 2 - 1)
            ffn_add(FT // 2)
            dve.wait_ge(gate_done, 1)
            nc.vector.memset(acc[:, :, :], 0.0).then_inc(zeroed, 1)

            def cos_part(g, bp, c):
                dve.wait_ge(swapped, cnt(5, g, bp, c + 1))
                wait(dve, scores_ps, cnt(8, g, bp, -8))
                dst = q[:, bp, c - 1, :] if c else k[:, bp, :]
                nc.vector.tensor_tensor(dst.rearrange("p (b n) -> p b n", b=2),
                                        PJ_B[(c + 1 if c else 0) % 2][:, :].rearrange("p (b n) -> p b n", b=2),
                                        spread(cos.unsqueeze(1), P, 2, SEQ), ALU.mult).then_inc(cos_done, 1)

            def rotate(g, bp, c):
                dve.wait_ge(sin_done, cnt(5, g, bp, c + 1))
                dve.wait_ge(cos_done, cnt(5, g, bp, c + 1))
                dst = q[:, bp, c - 1, :] if c else k[:, bp, :]
                nc.vector.tensor_tensor(dst, dst, swap[:, (5 * bp + c) % 2, :], ALU.add).then_inc(rope_done, 1)

            def negate(g, bp, b, h):
                s = 4 * b + h
                dve.wait_ge(masked, cnt(8, g, bp, s + 1))
                nc.vector.tensor_scalar(nmx[:, s, :], mx[:, s, :], -SM, None, ALU.mult).then_inc(nmax_done, 1)

            def masking(g, bp, b):
                wait(dve, pT_ps, cnt(6, g, bp, 3 * b - 3))
                for h in range(GH):
                    s = 4 * b + h
                    dve.wait_ge(scores_ps, cnt(8, g, bp, s + 1))
                    if h:
                        negate(g, bp, b, h - 1)
                    else:
                        nc.vector.memset(pace[:, b:b + 1], 0.0)
                    for i, (c0, c1) in enumerate(((0, P), (P, 3 * P))):
                        m = nc.vector.tensor_tensor_reduce(
                            out=probs[:, s, c0:c1], in0=S_B[s % 2][:, c0:c1], in1=mask[:, c0:c1], scale=1.0,
                            scalar=NEG, op0=ALU.add, op1=ALU.max, accum_out=mx[:, s, i:i + 1])
                    m.then_inc(masked, 1)
                negate(g, bp, b, GH - 1)

            def normalise(g, bp, b, h):
                s = 4 * b + h
                dve.wait_ge(exp_done, cnt(8, g, bp, s + 1))
                nc.vector.reciprocal(rinv[:, s, :], rsum[:, s, :]).then_inc(rinv_done, 1)
                dve.wait_ge(rinv_done, cnt(8, g, bp, s + 1))
                for i, (c0, c1) in enumerate(((0, P), (P, 3 * P))):
                    m = nc.vector.tensor_scalar(probs[:, s, c0:c1], probs[:, s, c0:c1], rinv[:, s, i:i + 1], None,
                                                ALU.mult)
                m.then_inc(probs_done, 1)

            def p_lo(g, bp, b, r):
                dve.wait_ge(ph_done, cnt(6, g, bp, 3 * b + r + 1))
                nc.vector.tensor_tensor(pl[:, r, :], T_B[(7 * bp + 4 * b + r) % 2][:, :], ph[:, r, :].bitcast(f32),
                                        ALU.subtract).then_inc(pl_done, 1)

            def v_lo(g, bp, t_bank):
                dve.wait_ge(vh_done, cnt(1, g, bp, 1))
                nc.vector.tensor_tensor(vl[:, bp].rearrange("p t n -> p (t n)"), t_bank[:, :],
                                        vh[:, bp].rearrange("p t n -> p (t n)").bitcast(f32),
                                        ALU.subtract).then_inc(vl_done, 1)

            def o_lo(g, bp, j):
                dve.wait_ge(oh_done, cnt(4, g, bp, j + 1))
                nc.vector.tensor_tensor(ol[:, j].rearrange("p h n -> p (h n)"), O_B[j % 2][:, :],
                                        oh[:, j].rearrange("p h n -> p (h n)").bitcast(f32),
                                        ALU.subtract).then_inc(ol_done, 1)

            def accumulate(g, bp, t):
                dve.wait_ge(y_ps, cnt(4, g, bp, t + 1))
                wait(dve, acc_done, cnt(4, g, bp, t - 7))
                a = acc[:, 4 * bp + t, :]
                nc.vector.tensor_tensor(a, a, O_B[t % 2][:, :], ALU.add).then_inc(acc_done, 1)

            cos_part(0, 0, 0)
            cos_part(0, 0, 1)
            rotate(0, 0, 0)
            v_lo(0, 0, T_B[1])
            cos_part(0, 0, 2)
            rotate(0, 0, 1)
            cos_part(0, 0, 3)
            rotate(0, 0, 2)
            cos_part(0, 0, 4)
            rotate(0, 0, 3)
            rotate(0, 0, 4)
            dve.wait_ge(zeroed, 6)
            dve.wait_ge(const_in, 16)
            masking(0, 0, 0)
            for h in range(GH):
                normalise(0, 0, 0, h)

            def step(g, bp, last):
                ng, nbp = (g, 1) if bp == 0 else (g + 1, 0)
                more = not (last and bp == 1)
                for r in range(3):
                    p_lo(g, bp, 0, r)
                if more:
                    cos_part(ng, nbp, 0)
                o_lo(g, bp, 0)
                o_lo(g, bp, 1)
                if more:
                    rotate(ng, nbp, 0)
                masking(g, bp, 1)
                if more:
                    cos_part(ng, nbp, 1)
                for h in range(GH):
                    normalise(g, bp, 1, h)
                if more:
                    v_lo(ng, nbp, T_B[(7 * bp + 3) % 2])
                    rotate(ng, nbp, 1)
                    cos_part(ng, nbp, 2)
                    cos_part(ng, nbp, 3)
                    rotate(ng, nbp, 2)
                for r in range(3):
                    p_lo(g, bp, 1, r)
                if more:
                    rotate(ng, nbp, 3)
                    cos_part(ng, nbp, 4)
                o_lo(g, bp, 2)
                o_lo(g, bp, 3)
                if more:
                    rotate(ng, nbp, 4)
                accumulate(g, bp, 0)
                if more:
                    masking(ng, nbp, 0)
                accumulate(g, bp, 1)
                if more:
                    for h in range(GH):
                        normalise(ng, nbp, 0, h)
                accumulate(g, bp, 2)
                accumulate(g, bp, 3)

            def group(g, last=False):
                step(g, 0, last)
                step(g, 1, last)

            group(0)
            with dve.Fori(1, NKV - 1) as g:
                group(g)
            group(NKV - 1, True)

            for t in range(NT):
                dve.wait_ge(acc_done, 8 * (NKV - 1) + t + 1)
                dve.wait_ge(gate_done, 2)
                nc.vector.tensor_tensor(acc[:, t, :], acc[:, t, :], gate[:, t, :], ALU.mult).then_inc(gated, 1)
                dve.wait_ge(gated, t + 1)
                w = ALL_W + t
                dve.wait_ge(raw_in[w % RING], 16 * (w // RING + 1))
                nc.vector.tensor_tensor(gate[:, t, :], acc[:, t, :], raw[:, w % RING, :], ALU.add).then_inc(final, 1)

        @block.tensor
        def _(pe):
            def three(out_, pairs):
                n = len(pairs)
                for i, (sh, sl, mh, ml) in enumerate(pairs):
                    nc.tensor.matmul(out_, sh, mh, start=(i == 0), stop=False)
                    nc.tensor.matmul(out_, sh, ml, start=False, stop=False)
                    m = nc.tensor.matmul(out_, sl, mh, start=False, stop=(i == n - 1))
                return m

            pe.wait_ge(const_in, 16)
            for i in range(NT):
                pe.wait_ge(xn_done, i + 1)
                wait(pe, xl_done, i - 3)
                for d in range(DT):
                    m = nc.tensor.transpose(bank[i % 4][:, d * P:(d + 1) * P], xn[:, i, d * P:(d + 1) * P], ident)
                m.then_inc(xT_ps, 1)

            def w13_turn(t, s2_):
                pe.wait_ge(W13_done, t + 1)
                for m in range(2):
                    wait(pe, W13l_done, 2 * t + (m - 1))
                    for d in range(DT):
                        i = nc.tensor.transpose(bank[m][:, d * P:(d + 1) * P],
                                                W13[:, s2_, m, d * P:(d + 1) * P], ident)
                    i.then_inc(W13_ps, 1)

            def w13_mult(t, s2_):
                for half in range(2):
                    wait(pe, h_done, 2 * t + (half - 1))
                    cols = slice(half * IT, half * IT + IT)
                    for m in range(2):
                        pe.wait_ge(W13l_done, 2 * t + (m + 1))
                        three(bank[2 + 2 * half + m][:, :],
                              [(W13h[:, s2_, m, d, :], W13l[:, s2_, m, d, :], xh[:, d, cols], xl[:, d, cols])
                               for d in range(DT)]).then_inc(ab_ps, 1)

            def w2_turn(t):
                rows = P if t < FT - 1 else FR
                wait(pe, ffn_read, t - 1)
                W2f = W2n[:, :, :, :].rearrange("p r n c -> p (r n c)")
                for j in range(4):
                    i = nc.tensor.transpose(bank[6 + t % 2][0:rows, j * P:(j + 1) * P],
                                            W2f[:, j * F + t * P:j * F + t * P + rows], ident)
                i.then_inc(W2_ps, 1)

            def w2_mult(u, pair):
                for i in range(NT):
                    if i == 0:
                        pe.wait_ge(hl_done, 4 * u + 2 * len(pair))
                    wait(pe, ffn_read, 8 * u + (FT + i - 1))
                    cols = slice(i * P, (i + 1) * P)
                    three(bank[6 + (FT + i) % 2][:, :],
                          [(hh[s][:, cols], hl[s][:, cols],
                            W2h[:, bass.ds(2 * u + e, 1), :].rearrange("p o d -> p (o d)"),
                            W2l[:, bass.ds(2 * u + e, 1), :].rearrange("p o d -> p (o d)"))
                           for e, s in enumerate(pair)]).then_inc(ffn_ps, 1)

            pe.wait_ge(xl_done, NT)
            w13_turn(0, 0)
            w13_turn(1, 1)
            w13_mult(0, 0)
            pe.wait_ge(W2_done, 4)
            for t in range(6):
                w2_turn(t)
            w13_turn(2, 0)
            w13_mult(1, 1)
            for t in range(6, FT):
                w2_turn(t)
            with pe.Fori(0, 2) as v:
                for j in range(4):
                    w13_turn(4 * v + (3 + j), (3 + j) % 2)
                    w13_mult(4 * v + (2 + j), (2 + j) % 2)
                    if j % 2:
                        w2_mult(2 * v + j // 2, (0, 1) if j == 1 else (2, 3))
            w13_mult(FT - 1, (FT - 1) % 2)
            w2_mult(FT // 2 - 1, (0, 1))
            w2_mult(FT // 2, (2,))

            def project(g, bp, c):
                if bp == 0:
                    pe.wait_ge(wl_done, in_chunk(g, c) + 1)
                if c == 3:
                    wait(pe, vT_done, cnt(1, g, bp, 1))
                else:
                    r = {0: -1, 1: 0, 2: 1, 4: 2, 5: 3}[c]
                    wait(pe, cos_done, cnt(5, g, bp, r))
                cols = slice(bp * IT, bp * IT + IT)
                three(PJ_B[c % 2][:, :],
                      [(wih[:, c, d, :], wil[:, c, d, :], xh[:, d, cols], xl[:, d, cols])
                       for d in range(DT)]).then_inc(proj_ps, 1)

            def v_turn(g, bp, t_bank):
                pe.wait_ge(vT_done, cnt(1, g, bp, 1))
                for t in range(IT // P):
                    i = nc.tensor.transpose(t_bank[:, t * P:(t + 1) * P], vT[:, t * P:(t + 1) * P], ident)
                i.then_inc(v_ps, 1)

            def scores(g, bp, b, h):
                s = 4 * b + h
                if b == 0:
                    pe.wait_ge(rope_done, cnt(5, g, bp, h + 2))
                wait(pe, masked, cnt(8, g, bp, s - 1))
                c = b * SEQ
                nc.tensor.matmul(S_B[s % 2][:, 0:P], q[:, bp, h, c:c + P], k[:, bp, c:c + P], start=True, stop=True)
                nc.tensor.matmul(S_B[s % 2][:, P:3 * P], q[:, bp, h, c + P:c + SEQ], k[:, bp, c:c + SEQ],
                                 start=True, stop=True).then_inc(scores_ps, 1)

            def p_turn(g, bp, b, r, last):
                j = 4 * b + r
                if r == 0:
                    pe.wait_ge(probs_done, cnt(8, g, bp, 4 * b + 4))
                if j == 5:
                    if last:
                        pe.wait_ge(pl_done, cnt(6, g, bp, 2))
                    else:
                        pe.wait_ge(vl_done, cnt(1, g, bp, 2))
                else:
                    wait(pe, pl_done, cnt(6, g, bp, {0: -1, 1: 0, 2: 1, 4: 3, 6: 4}[j]))
                    if j == 1:
                        pe.wait_ge(vl_done, cnt(1, g, bp, 1))
                for h in range(GH):
                    i = nc.tensor.transpose(T_B[(7 * bp + j) % 2][:, h * P:(h + 1) * P],
                                            probs[:, 4 * b + h, r * P:(r + 1) * P], ident)
                i.then_inc(pT_ps, 1)

            def attend(g, bp, b):
                pe.wait_ge(vl_done, cnt(1, g, bp, 1))
                for t in range(2):
                    j = 2 * b + t
                    if b == 0:
                        wait(pe, acc_done, cnt(4, g, bp, t - 1))
                    else:
                        pe.wait_ge(ol_done, cnt(4, g, bp, t + 1))
                    blocks = ((0, 0),) if t == 0 else ((1, 0), (2, 1))
                    pe.wait_ge(pl_done, cnt(6, g, bp, 3 * b + (1 if t == 0 else 3)))
                    three(O_B[j % 2][:, :], [(vh[:, bp, 2 * b + kt, :], vl[:, bp, 2 * b + kt, :],
                                              ph[:, r, :], pl[:, r, :]) for r, kt in blocks]).then_inc(o_ps, 1)

            def out_project(g, bp, t):
                pe.wait_ge(ol_done, cnt(4, g, bp, t + 1 if t > 1 else t + 3))
                if t > 1:
                    pe.wait_ge(acc_done, cnt(4, g, bp, t - 1))
                if bp == 0 and t == 0:
                    pe.wait_ge(wl_done, wo_chunk(g, GH - 1) + 1)
                three(O_B[t % 2][:, :], [(oh[:, t, h, :], ol[:, t, h, :], woh[:, h, :], wol[:, h, :])
                                         for h in range(GH)]).then_inc(y_ps, 1)

            pe.wait_ge(gate_done, 1)
            pe.wait_ge(ffn_read, FT + 6 * NT)
            project(0, 0, 0)
            project(0, 0, 1)
            project(0, 0, 2)
            v_turn(0, 0, T_B[1])
            for c in range(3, 6):
                project(0, 0, c)
            for h in range(GH):
                scores(0, 0, 0, h)

            def step(g, bp, last):
                ng, nbp = (g, 1) if bp == 0 else (g + 1, 0)
                more = not (last and bp == 1)
                for r in range(3):
                    p_turn(g, bp, 0, r, not more)
                if more:
                    project(ng, nbp, 0)
                    project(ng, nbp, 1)
                attend(g, bp, 0)
                for h in range(GH):
                    scores(g, bp, 1, h)
                if more:
                    project(ng, nbp, 2)
                    pe.wait_ge(pl_done, cnt(6, g, bp, 2))
                    v_turn(ng, nbp, T_B[(7 * bp + 3) % 2])
                    project(ng, nbp, 3)
                    project(ng, nbp, 4)
                for r in range(3):
                    p_turn(g, bp, 1, r, not more)
                if more:
                    project(ng, nbp, 5)
                attend(g, bp, 1)
                out_project(g, bp, 0)
                if more:
                    for h in range(GH):
                        scores(ng, nbp, 0, h)
                for t in range(1, 4):
                    out_project(g, bp, t)

            def group(g, last=False):
                step(g, 0, last)
                step(g, 1, last)

            group(0)
            with pe.Fori(1, NKV - 1) as g:
                group(g)
            group(NKV - 1, True)


def constants():
    inv = (np.float32(10000.0) ** (-np.arange(HALF, dtype=np.float32) / np.float32(HALF))).astype(np.float32)
    ang = np.arange(SEQ, dtype=np.float32)[None, :] * inv[:, None]
    cos, sin = np.cos(ang), np.sin(ang)
    c = np.zeros((P, C_W), np.float32)
    c[:, C_COS:C_COS + SEQ] = np.concatenate([cos, cos])
    c[:, C_SIN:C_SIN + SEQ] = np.concatenate([-sin, sin])
    i, j = np.arange(P)[:, None], np.arange(P)[None, :]
    for n, ok in enumerate((j <= i, j > i, j <= i)):
        c[:, C_MASK + n * P:C_MASK + (n + 1) * P] = np.where(ok, 0.0, NEG)
    c[:, C_ID:C_ID + P] = np.eye(P)
    return c


_INS = ["L0_attn_x", "L0_attn_wq", "L0_attn_wk", "L0_attn_wv", "L0_attn_wo",
        "L0_ffn_w1", "L0_ffn_s1", "L0_ffn_w2", "L0_ffn_s2", "L0_ffn_w3", "L0_ffn_s3"]


def kernel(**inputs):
    import numpy as _np
    import concourse.bacc as _bacc
    from concourse import mybir as _mybir
    from concourse.bass_utils import run_bass_kernel_spmd as _run

    nc = _bacc.Bacc("TRN2", target_bir_lowering=False, num_devices=1)
    arrays, args = {}, []
    for name, a in [(n, inputs[n]) for n in _INS] + [("constants", constants())]:
        a = _np.ascontiguousarray(a)
        arrays[f"in_{name}"] = a
        args.append(nc.dram_tensor(f"in_{name}", a.shape, _mybir.dt.from_np(a.dtype), kind="ExternalInput").ap())
    args.append(nc.dram_tensor("out_0", (B, SEQ, D), _mybir.dt.float32, kind="ExternalOutput").ap())
    build(nc, *args)
    r = _run(nc, [arrays], core_ids=[0])
    return r.results[0]["out_0"]
```

```python
from contextlib import ExitStack

import numpy as np
import concourse.bass as bass
from concourse import mybir

B, SEQ, D = 4, 256, 512
HD, NQ, NKV = 128, 32, 8
GH = NQ // NKV
HALF = HD // 2
F = 1376
GROUP = 64
P = 128
TOK = B * SEQ
NT = TOK // P
DT = D // P
IT = 512
FT = -(-F // P)
FR = F - (FT - 1) * P
PK = D // 2
R2 = F * D // 2 // GROUP // P
EPS = 1e-5
SM = float(HD) ** -0.5
NEG = -3.0e38
RING = 5
CHUNKS = 6 + GH
ALL_W = CHUNKS * NKV
C_COS, C_SIN, C_MASK, C_ID, C_W = 0, SEQ, 2 * SEQ, 2 * SEQ + 3 * P, 2 * SEQ + 4 * P


def build(nc, x, wq, wk, wv, wo, w1, s1, w2, s2, w3, s3, const, out):
    f32, f32r, i32 = mybir.dt.float32, mybir.dt.float32r, mybir.dt.int32
    ALU, ACT = mybir.AluOpType, mybir.ActivationFunctionType

    x_v = x.rearrange("b (t p) d -> p (b t) d", p=P)
    out_v = out.rearrange("b (t p) d -> p (b t) d", p=P)
    wq_v = wq.rearrange("(t p) n -> p t n", p=P)
    wk_v = wk.rearrange("(t p) n -> p t n", p=P)
    wv_v = wv.rearrange("(t p) n -> p t n", p=P)
    w13_v = [w.rearrange("(h r) c -> h (r c)", r=PK // GROUP) for w in (w1, w3)]
    s13_v = [s.rearrange("(h g) -> h g", g=D // GROUP) for s in (s1, s3)]
    w2_v = w2.rearrange("(p r) c -> p (r c)", r=R2)
    s2_v = s2.rearrange("(p g) -> p g", g=2 * R2)

    ctx = ExitStack()
    with ctx:
        def sb(name, shape, dt, at=ctx):
            return at.enter_context(nc.sbuf_tensor(name, shape, dt))

        def sem(name):
            return ctx.enter_context(nc.semaphore(name))

        gate = sb("gate", [P, NT, D], f32)
        cst = sb("cst", [P, C_W], f32)
        cos, sin = cst[:, C_COS:C_COS + SEQ], cst[:, C_SIN:C_SIN + SEQ]
        mask, ident = cst[:, C_MASK:C_MASK + 3 * P], cst[:, C_ID:C_ID + P]
        raw = sb("raw", [P, RING, D], f32)
        xh = sb("xh", [P, DT, TOK], f32r)
        xl = sb("xl", [P, DT, TOK], f32r)
        main = ctx.enter_context(ExitStack())

        ffn = ctx.enter_context(ExitStack())
        packed = sb("packed", [P, 4, 2, PK], i32, ffn)
        s13 = sb("s13", [P, FT, 2, D // GROUP], f32, ffn)
        nib = sb("nib", [P, 2, 2 * PK], i32, ffn)
        W13 = sb("W13", [P, 2, 2, D], f32, ffn)
        W13h = sb("W13h", [P, 2, 2, DT, P], f32r, ffn)
        W13l = sb("W13l", [P, 2, 2, DT, P], f32r, ffn)
        NR2 = 11
        packed2 = sb("packed2", [P, 2, NR2 * GROUP], i32, ffn)
        nib2 = sb("nib2", [P, 2, NR2 * GROUP], i32, ffn)
        s2s = sb("s2s", [P, 2 * R2], f32, ffn)
        stat = sb("stat", [P, NT, 6], f32, ffn)
        mv = sb("mv", [P, NT, 2], f32, ffn)
        std = sb("std", [P, 4, NT], f32, ffn)
        act_h = sb("act_h", [P, 2, IT], f32, ffn)
        early = ffn.enter_context(ExitStack())
        xn = sb("xn", [P, NT, D], f32, early)
        W2n = sb("W2n", [P, R2, 2, GROUP], f32, early)
        early.close()
        hid_hl = sb("hid_hl", [P, 2, 2, 2, TOK], f32r, ffn)
        gap = sb("gap", [P, R2 * 2 * GROUP + NT * D - 8 * TOK], f32, ffn)
        W2h = sb("W2h", [P, FT, D], f32r, ffn)
        W2l = sb("W2l", [P, FT, D], f32r, ffn)
        hh = [hid_hl[:, s // 2, 0, s % 2, :] for s in range(4)]
        hl = [hid_hl[:, s // 2, 1, s % 2, :] for s in range(4)]
        ffn.close()

        wih = sb("wih", [P, 6, DT, P], f32r, main)
        wil = sb("wil", [P, 6, DT, P], f32r, main)
        swap = sb("swap", [P, 2, IT], f32, main)
        vT = sb("vT", [P, IT], f32, main)
        k = sb("k", [P, 2, IT], f32, main)
        q = sb("q", [P, 2, GH, IT], f32, main)
        probs = sb("probs", [P, 2 * GH, 3 * P], f32, main)
        vh = sb("vh", [P, 2, IT // P, HD], f32r, main)
        vl = sb("vl", [P, 2, IT // P, HD], f32r, main)
        mx = sb("mx", [P, 2 * GH, 2], f32, main)
        pace = sb("pace", [P, 4], f32, main)
        nmx = sb("nmx", [P, 2 * GH, 2], f32, main)
        rsum = sb("rsum", [P, 2 * GH, 2], f32, main)
        rinv = sb("rinv", [P, 2 * GH, 2], f32, main)
        ph = sb("ph", [P, 3, GH * P], f32r, main)
        pl = sb("pl", [P, 3, GH * P], f32r, main)
        oh = sb("oh", [P, 4, GH, P], f32r, main)
        ol = sb("ol", [P, 4, GH, P], f32r, main)
        woh = sb("woh", [P, GH, D], f32r, main)
        wol = sb("wol", [P, GH, D], f32r, main)
        acc = sb("acc", [P, NT, D], f32, main)

        bank = [ctx.enter_context(nc.psum_tensor(f"bank{i}", [P, 512], f32)) for i in range(8)]
        S_B, PJ_B, T_B, O_B = bank[0:2], bank[2:4], bank[4:6], bank[6:8]

        const_in, s13_in, s2_in, out_done = sem("const_in"), sem("s13_in"), sem("s2_in"), sem("out_done")
        x_in = [sem(f"x_in{i}") for i in range(4)]
        w13_in = [sem(f"w13_in{i}") for i in range(4)]
        w2_in = [sem(f"w2_in{i}") for i in range(2)]
        raw_in = [sem(f"raw_in{i}") for i in range(RING)]
        zeroed, stats_done, mv_done, ln_small, std_done = (
            sem("zeroed"), sem("stats_done"), sem("mv_done"), sem("ln_small"), sem("std_done"))
        xn_done, xT_ps, xh_done, xl_done = sem("xn_done"), sem("xT_ps"), sem("xh_done"), sem("xl_done")
        nib_done, W13_done, W13_ps, W13h_done, W13l_done = (
            sem("nib_done"), sem("W13_done"), sem("W13_ps"), sem("W13h_done"), sem("W13l_done"))
        nib2_done, W2_done, W2_ps, W2h_done = sem("nib2_done"), sem("W2_done"), sem("W2_ps"), sem("W2h_done")
        ab_ps, silu_done, h_done, hh_done, hl_done = (
            sem("ab_ps"), sem("silu_done"), sem("h_done"), sem("hh_done"), sem("hl_done"))
        ffn_ps, ffn_read, gate_done = sem("ffn_ps"), sem("ffn_read"), sem("gate_done")
        scores_ps, masked, nmax_done, exp_done, rinv_done, probs_done = (
            sem("scores_ps"), sem("masked"), sem("nmax_done"), sem("exp_done"), sem("rinv_done"),
            sem("probs_done"))
        proj_ps, cos_done, swapped, sin_done, rope_done = (
            sem("proj_ps"), sem("cos_done"), sem("swapped"), sem("sin_done"), sem("rope_done"))
        vT_done, v_ps, vh_done, vl_done = sem("vT_done"), sem("v_ps"), sem("vh_done"), sem("vl_done")
        pT_ps, ph_done, pl_done = sem("pT_ps"), sem("ph_done"), sem("pl_done")
        o_ps, oh_done, ol_done = sem("o_ps"), sem("oh_done"), sem("ol_done")
        y_ps, acc_done = sem("y_ps"), sem("acc_done")
        wh_done, wl_done = sem("wh_done"), sem("wl_done")
        rest_mul, rest_done = sem("rest_mul"), sem("rest_done")
        gated, final = sem("gated"), sem("final")

        def wait(eng, s, value):
            if isinstance(value, int) and value <= 0:
                return
            eng.wait_ge(s, value)

        def cnt(per, g, bp, c):
            return 2 * per * g + (per * bp + c)

        def spread(ap, *sizes):
            return ap.to_broadcast(list(sizes))

        block = ctx.enter_context(nc.Block())

        def wo_chunk(g, h):
            return CHUNKS * g + (6 + h)

        def in_chunk(g, c):
            return CHUNKS * g + c

        @block.sync
        def _(sp):
            for i in range(4):
                sp.dma_start(xn[:, 2 * i:2 * i + 2, :], x_v[:, 2 * i:2 * i + 2, :]).then_inc(x_in[i], 16)
                if i == 0:
                    sp.dma_start(cst[:, :], const).then_inc(const_in, 16)

            def load13(t):
                rows = P if t < FT - 1 else FR
                wait(sp, nib_done, t - 3)
                for m in range(2):
                    sp.dma_start(packed[0:rows, t % 4, m, :], w13_v[m][t * P:t * P + rows, :]) \
                        .then_inc(w13_in[t % 4], 16)

            sp.wait_ge(zeroed, 2)
            for m in range(2):
                sp.dma_start(s13[:, 0:FT - 1, m, :],
                             s13_v[m][0:(FT - 1) * P, :].rearrange("(t p) g -> p t g", p=P)).then_inc(s13_in, 16)
                sp.dma_start(s13[0:FR, FT - 1, m, :], s13_v[m][(FT - 1) * P:F, :]).then_inc(s13_in, 16)
            load13(0)
            load13(1)
            sp.dma_start(s2s[:, :], s2_v).then_inc(s2_in, 16)
            for i in range(4):
                r0, r1 = NR2 * i, min(NR2 * i + NR2, R2)
                wait(sp, nib2_done, i - 1)
                sp.dma_start(packed2[:, i % 2, 0:(r1 - r0) * GROUP],
                             w2_v[:, r0 * GROUP:r1 * GROUP]).then_inc(w2_in[i % 2], 16)
                if i < 2:
                    load13(2 + i)
            for t in range(4, FT):
                load13(t)

            def load_in(w, g, c):
                src = (wk_v, wv_v)[c][:, :, bass.ds(g * HD, HD)] if c < 2 else \
                    wq_v[:, :, bass.ds(g * (GH * HD) + (c - 2) * HD, HD)]
                s = w if isinstance(w, int) else c + CHUNKS
                sp.dma_start(raw[:, s % RING, :].rearrange("p (t n) -> p t n", t=DT), src) \
                    .then_inc(raw_in[s % RING], 16)

            for c in range(6):
                wait(sp, wl_done, c - RING + 1)
                load_in(c, 0, c)

            def group_loads(g, last):
                for h in range(GH):
                    wait(sp, wl_done, wo_chunk(g, h) - RING + 1)
                    sp.dma_start(raw[:, (6 + h) % RING, :], wo[bass.ds(g * (GH * HD) + h * HD, HD), :]) \
                        .then_inc(raw_in[(6 + h) % RING], 16)
                if not last:
                    for c in range(6):
                        wait(sp, wl_done, in_chunk(g + 1, c) - RING + 1)
                        load_in(None, g + 1, c)

            group_loads(0, False)
            with sp.Fori(1, NKV - 1) as g:
                group_loads(g, False)
            group_loads(NKV - 1, True)
            for t in range(NT + RING):
                if t < NT:
                    if t < RING:
                        sp.wait_ge(wl_done, ALL_W + t - RING + 1)
                    else:
                        sp.wait_ge(rest_done, t - RING + 1)
                    sp.dma_start(raw[:, (ALL_W + t) % RING, :], x_v[:, t, :]).then_inc(raw_in[(ALL_W + t) % RING], 16)
                if t >= RING:
                    sp.wait_ge(final, t - RING + 1)
                    sp.dma_start(out_v[:, t - RING, :], gate[:, t - RING, :]).then_inc(out_done, 16)
            sp.wait_ge(out_done, 16 * NT)

        @block.gpsimd
        def _(pool):
            def hid_lo(t, s4):
                for half in range(2):
                    pool.wait_ge(hh_done, 2 * t + (half + 1))
                    cols = slice(half * IT, half * IT + IT)
                    nc.gpsimd.tensor_tensor(hl[s4][:, cols], act_h[:, half, :], hh[s4][:, cols].bitcast(f32),
                                            ALU.subtract).then_inc(hl_done, 1)

            for t in range(2):
                hid_lo(t, t)
            with pool.Fori(0, 2) as v:
                for j in range(4):
                    hid_lo(4 * v + (2 + j), (2 + j) % 4)
            hid_lo(FT - 1, (FT - 1) % 4)

            def w_lo(w, slot, hi, lo):
                pool.wait_ge(wh_done, w + 1)
                nc.gpsimd.tensor_tensor(lo, raw[:, slot, :], hi.bitcast(f32), ALU.subtract).then_inc(wl_done, 1)

            def flat(ap):
                return ap.rearrange("p t n -> p (t n)")

            def lo_in(g, c):
                w_lo(in_chunk(g, c), c % RING, flat(wih[:, c]), flat(wil[:, c]))

            def lo_wo(g, h):
                w_lo(wo_chunk(g, h), (6 + h) % RING, woh[:, h, :], wol[:, h, :])

            def sin_part(g, bp, c):
                s = (5 * bp + c) % 2
                pool.wait_ge(swapped, cnt(5, g, bp, c + 1))
                v = swap[:, s, :].rearrange("p (b n) -> p b n", b=2)
                nc.gpsimd.tensor_tensor(v, v, spread(sin.unsqueeze(1), P, 2, SEQ), ALU.mult).then_inc(sin_done, 1)

            pool.wait_ge(ab_ps, 4 * FT)
            for c in range(6):
                lo_in(0, c)
            for c in range(5):
                sin_part(0, 0, c)

            def rest(t):
                pool.wait_ge(acc_done, 8 * (NKV - 2) + t + 1)
                pool.wait_ge(gate_done, NT)
                nc.gpsimd.tensor_tensor(acc[:, t, :], acc[:, t, :], gate[:, t, :], ALU.mult).then_inc(rest_mul, 1)
                w = ALL_W + t
                pool.wait_ge(rest_mul, t + 1)
                pool.wait_ge(raw_in[w % RING], 16 * (w // RING + 1))
                nc.gpsimd.tensor_tensor(acc[:, t, :], acc[:, t, :], raw[:, w % RING, :], ALU.add) \
                    .then_inc(rest_done, 1)

            def step(g, bp, last):
                ng, nbp = (g, 1) if bp == 0 else (g + 1, 0)
                more = not (last and bp == 1)
                w = bp == 0
                nxt = w and not last
                if not more:
                    for t in range(4, NT):
                        rest(t)
                    return
                if more:
                    sin_part(ng, nbp, 0)
                if w:
                    lo_wo(g, 0)
                    lo_wo(g, 1)
                    lo_wo(g, 2)
                    lo_wo(g, 3)
                for c in range(1, 5):
                    sin_part(ng, nbp, c)
                    if nxt:
                        lo_in(g + 1, c - 1)
                    elif w:
                        rest(c - 1)
                if nxt:
                    lo_in(g + 1, 4)
                    lo_in(g + 1, 5)

            def group(g, last=False):
                step(g, 0, last)
                step(g, 1, last)

            group(0)
            with pool.Fori(1, NKV - 1) as g:
                group(g)
            group(NKV - 1, True)

        @block.scalar
        def _(act):
            act.wait_ge(ln_small, 1)
            nc.scalar.activation(std[:, 1, :], std[:, 0, :], ACT.Sqrt).then_inc(std_done, 1)
            for i in range(NT):
                act.wait_ge(xT_ps, i + 1)
                nc.scalar.activation(xh[:, :, i * P:(i + 1) * P],
                                     bank[i % 4][:, :].rearrange("p (t n) -> p t n", t=DT),
                                     ACT.Copy).then_inc(xh_done, 1)

            def w13_hi(t, s2_):
                for m in range(2):
                    act.wait_ge(W13_ps, 2 * t + (m + 1))
                    wait(act, ab_ps, 4 * t - 4)
                    nc.scalar.activation(W13h[:, s2_, m].rearrange("p t n -> p (t n)"), bank[m][:, :],
                                         ACT.Copy).then_inc(W13h_done, 1)

            def hidden(t, u, s4):
                for half in range(2):
                    act.wait_ge(ab_ps, 4 * t + (2 * half + 1))
                    wait(act, hl_done, 2 * t + (half - 1))
                    nc.scalar.activation(act_h[:, half, :], bank[2 + 2 * half][:, :], ACT.Silu) \
                        .then_inc(silu_done, 1)
                for half in range(2):
                    act.wait_ge(h_done, 2 * t + (half + 1))
                    if not isinstance(u, int) or u:
                        act.wait_ge(ffn_read, 8 * u + (FT - 8))
                    nc.scalar.activation(hh[s4][:, half * IT:half * IT + IT], act_h[:, half, :],
                                         ACT.Copy).then_inc(hh_done, 1)

            def w2_hi(t):
                act.wait_ge(W2_ps, t + 1)
                nc.scalar.activation(W2h[:, t, :].rearrange("h (p j) -> h j p", j=4)[0:(P if t < FT - 1 else FR)],
                                     bank[6 + t % 2][0:(P if t < FT - 1 else FR), :]
                                     .rearrange("h (j p) -> h j p", j=4), ACT.Copy).then_inc(W2h_done, 1)

            w13_hi(0, 0)
            w13_hi(1, 1)
            hidden(0, 0, 0)
            for t in range(6):
                w2_hi(t)
            w13_hi(2, 0)
            hidden(1, 0, 1)
            for t in range(6, FT):
                w2_hi(t)
            with act.Fori(0, 2) as v:
                for j in range(4):
                    w13_hi(4 * v + (3 + j), (3 + j) % 2)
                    hidden(4 * v + (2 + j), 2 * v + (1 + j // 2), (2 + j) % 4)
            hidden(FT - 1, FT // 2, (FT - 1) % 4)
            def w_hi(slot, use, hi):
                act.wait_ge(raw_in[slot], 16 * use)
                nc.scalar.activation(hi, raw[:, slot, :], ACT.Copy).then_inc(wh_done, 1)

            def hi_in(g, c):
                wait(act, proj_ps, cnt(6, g, -1, c + 1))
                w_hi(c % RING, 2 * g + (c // RING + 1), wih[:, c].rearrange("p t n -> p (t n)"))

            def hi_wo(g, h):
                wait(act, y_ps, 8 * g)
                w_hi((6 + h) % RING, 2 * g + ((6 + h) // RING + 1), woh[:, h, :])

            def halves(g, bp, c):
                a = 5 * bp + c
                act.wait_ge(proj_ps, cnt(6, g, bp, (c + 2 if c else 1)))
                wait(act, rope_done, cnt(5, g, bp, c - 1))
                src = PJ_B[(c + 1 if c else 0) % 2]
                nc.scalar.activation(swap[0:HALF, a % 2, :], src[HALF:P, :], ACT.Copy)
                nc.scalar.activation(swap[HALF:P, a % 2, :], src[0:HALF, :], ACT.Copy).then_inc(swapped, 1)

            def v_out(g, bp):
                act.wait_ge(proj_ps, cnt(6, g, bp, 2))
                wait(act, v_ps, cnt(1, g, bp, 0))
                nc.scalar.activation(vT[:, :], PJ_B[1][:, :], ACT.Copy).then_inc(vT_done, 1)

            def v_hi(g, bp, t_bank):
                act.wait_ge(v_ps, cnt(1, g, bp, 1))
                wait(act, o_ps, cnt(4, g, bp, -4))
                nc.scalar.activation(vh[:, bp].rearrange("p t n -> p (t n)"), t_bank[:, :],
                                     ACT.Copy).then_inc(vh_done, 1)

            def exps(g, bp, b, h):
                s = 4 * b + h
                act.wait_ge(nmax_done, cnt(8, g, bp, s + 1))
                for i, (c0, c1) in enumerate(((0, P), (P, 3 * P))):
                    e = nc.scalar.activation(probs[:, s, c0:c1], probs[:, s, c0:c1], ACT.Exp,
                                             bias=nmx[:, s, i:i + 1], scale=SM, accum_out=rsum[:, s, i:i + 1])
                e.then_inc(exp_done, 1)

            def p_hi(g, bp, b, r):
                j = 4 * b + r
                act.wait_ge(pT_ps, cnt(6, g, bp, 3 * b + r + 1))
                wait(act, o_ps, cnt(4, g, bp, 2 * b))
                nc.scalar.activation(ph[:, r, :], T_B[(7 * bp + j) % 2][:, :], ACT.Copy).then_inc(ph_done, 1)

            def o_hi(g, bp, j):
                act.wait_ge(o_ps, cnt(4, g, bp, j + 1))
                wait(act, y_ps, cnt(4, g, bp, j - 3))
                nc.scalar.activation(oh[:, j].rearrange("p h n -> p (h n)"), O_B[j % 2][:, :],
                                     ACT.Copy).then_inc(oh_done, 1)

            def gates(tiles):
                for t in tiles:
                    act.wait_ge(ffn_read, FT + 5 * NT + t + 1)
                    nc.scalar.activation(gate[:, t, :], gate[:, t, :], ACT.Silu).then_inc(gate_done, 1)

            act.wait_ge(ab_ps, 4 * FT)
            for c in range(6):
                hi_in(0, c)
            halves(0, 0, 0)
            v_out(0, 0)
            gates(range(4))
            halves(0, 0, 1)
            v_hi(0, 0, T_B[1])
            gates(range(4, NT))
            for c in range(2, 5):
                halves(0, 0, c)
            for h in range(GH):
                exps(0, 0, 0, h)

            def step(g, bp, last):
                ng, nbp = (g, 1) if bp == 0 else (g + 1, 0)
                more = not (last and bp == 1)
                w = bp == 0
                nxt = w and not last
                if not more:
                    for b in range(2):
                        for r in range(3):
                            p_hi(g, bp, b, r)
                        o_hi(g, bp, 2 * b)
                        o_hi(g, bp, 2 * b + 1)
                    return
                for r in range(3):
                    p_hi(g, bp, 0, r)
                if more:
                    halves(ng, nbp, 0)
                    v_out(ng, nbp)
                if w:
                    hi_wo(g, 0)
                    hi_wo(g, 1)
                o_hi(g, bp, 0)
                o_hi(g, bp, 1)
                if w:
                    hi_wo(g, 2)
                    hi_wo(g, 3)
                exps(g, bp, 1, 0)
                exps(g, bp, 1, 1)
                if more:
                    halves(ng, nbp, 1)
                exps(g, bp, 1, 2)
                exps(g, bp, 1, 3)
                if more:
                    v_hi(ng, nbp, T_B[(7 * bp + 3) % 2])
                if nxt:
                    hi_in(g + 1, 0)
                if more:
                    halves(ng, nbp, 2)
                if nxt:
                    hi_in(g + 1, 1)
                if more:
                    halves(ng, nbp, 3)
                for r in range(3):
                    p_hi(g, bp, 1, r)
                if nxt:
                    hi_in(g + 1, 2)
                if more:
                    halves(ng, nbp, 4)
                o_hi(g, bp, 2)
                o_hi(g, bp, 3)
                if nxt:
                    hi_in(g + 1, 3)
                if more:
                    for h in range(GH):
                        exps(ng, nbp, 0, h)
                if last:
                    for h in range(GH):
                        exps(ng, nbp, 1, h)
                if nxt:
                    hi_in(g + 1, 4)
                    hi_in(g + 1, 5)

            def group(g, last=False):
                step(g, 0, last)
                step(g, 1, last)

            group(0)
            with act.Fori(1, NKV - 1) as g:
                group(g)
            group(NKV - 1, True)

        @block.vector
        def _(dve):
            nc.vector.memset(s13[:, FT - 1, :, :], 0.0).then_inc(zeroed, 1)
            nc.vector.memset(packed[:, (FT - 1) % 4, :, :], 0).then_inc(zeroed, 1)
            nc.vector.memset(W2h[FR:P, FT - 1, :].bitcast(f32), 0.0).then_inc(zeroed, 1)
            nc.vector.memset(W2l[FR:P, FT - 1, :].bitcast(f32), 0.0).then_inc(zeroed, 1)

            for i in range(NT):
                dve.wait_ge(x_in[i // 2], 16)
                nc.vector.bn_stats(stat[:, i, :], xn[:, i, :]).then_inc(stats_done, 1)
            for i in range(NT):
                dve.wait_ge(stats_done, i + 1)
                nc.vector.bn_aggr(mv[:, i, :], stat[:, i, :]).then_inc(mv_done, 1)
            dve.wait_ge(mv_done, NT)
            nc.vector.tensor_scalar(std[:, 0, :], mv[:, :, 1], EPS, None, ALU.add).then_inc(ln_small, 1)
            dve.wait_ge(std_done, 1)
            nc.vector.reciprocal(std[:, 2, :], std[:, 1, :]).then_inc(ln_small, 1)
            dve.wait_ge(ln_small, 2)
            nc.vector.tensor_tensor(std[:, 3, :], std[:, 2, :], std[:, 2, :], ALU.mult).then_inc(ln_small, 1)
            dve.wait_ge(ln_small, 3)
            nc.vector.tensor_tensor(std[:, 1, :], std[:, 3, :], std[:, 0, :], ALU.mult).then_inc(ln_small, 1)
            dve.wait_ge(ln_small, 4)
            nc.vector.tensor_scalar(std[:, 3, :], std[:, 1, :], -0.5, 1.5, ALU.mult, ALU.add).then_inc(ln_small, 1)
            dve.wait_ge(ln_small, 5)
            nc.vector.tensor_tensor(std[:, 1, :], std[:, 3, :], std[:, 2, :], ALU.mult).then_inc(ln_small, 1)
            dve.wait_ge(ln_small, 6)
            for i in range(NT):
                nc.vector.tensor_scalar(xn[:, i, :], xn[:, i, :], mv[:, i, 0:1], std[:, 1, i:i + 1],
                                        ALU.subtract, ALU.mult).then_inc(xn_done, 1)

            def x_lo(i):
                dve.wait_ge(xh_done, i + 1)
                cols = slice(i * P, (i + 1) * P)
                nc.vector.tensor_tensor(xl[:, :, cols], bank[i % 4][:, :].rearrange("p (t n) -> p t n", t=DT),
                                        xh[:, :, cols].bitcast(f32), ALU.subtract).then_inc(xl_done, 1)

            def dequant13(t, s4, use):
                dve.wait_ge(w13_in[s4], 32 * use)
                wait(dve, W13_done, t)
                src = packed[:, s4].rearrange("p m c -> p (m c)")
                nc.vector.tensor_scalar(nib[:, 0, :], src, 4, None, ALU.arith_shift_right)
                nc.vector.tensor_scalar(nib[:, 1, :], src, 15, 8, ALU.bitwise_and, ALU.bitwise_xor) \
                    .then_inc(nib_done, 1)
                dve.wait_ge(nib_done, t + 1)
                wait(dve, W13_ps, 2 * t - 2)
                n = [nib[:, i, :].rearrange("p (g c) -> p g c", c=GROUP) for i in range(2)]
                sc = s13[:, bass.ds(t, 1), :, :].rearrange("p o m (g n) -> p n (o m g)", n=2)
                o = W13[:, s4 % 2].rearrange("p m (g n c) -> p n (m g) c", n=2, c=GROUP)
                GS = 2 * DT
                nc.vector.tensor_tensor(o[:, 0], n[0], spread(sc[:, 0].unsqueeze(2), P, GS, GROUP), ALU.mult)
                nc.vector.scalar_tensor_tensor(out=o[:, 1], in0=n[1], scalar=-8.0,
                                               in1=spread(sc[:, 1].unsqueeze(2), P, GS, GROUP),
                                               op0=ALU.add, op1=ALU.mult).then_inc(W13_done, 1)

            def w13_lo(t, s2_):
                for m in range(2):
                    dve.wait_ge(W13h_done, 2 * t + (m + 1))
                    nc.vector.tensor_tensor(W13l[:, s2_, m].rearrange("p t n -> p (t n)"), bank[m][:, :],
                                            W13h[:, s2_, m].rearrange("p t n -> p (t n)").bitcast(f32),
                                            ALU.subtract).then_inc(W13l_done, 1)

            def hid(t):
                for half in range(2):
                    dve.wait_ge(silu_done, 2 * t + (half + 1))
                    dve.wait_ge(ab_ps, 4 * t + (2 * half + 2))
                    nc.vector.tensor_tensor(act_h[:, half, :], act_h[:, half, :], bank[3 + 2 * half][:, :],
                                            ALU.mult).then_inc(h_done, 1)

            def dequant2(i):
                r0, r1 = NR2 * i, min(NR2 * i + NR2, R2)
                n = r1 - r0
                dve.wait_ge(w2_in[i % 2], 16 * (i // 2 + 1))
                wait(dve, W2_done, i)
                src = packed2[:, i % 2, 0:n * GROUP]
                nc.vector.tensor_scalar(nib2[:, 0, 0:n * GROUP], src, 4, None, ALU.arith_shift_right)
                nc.vector.tensor_scalar(nib2[:, 1, 0:n * GROUP], src, 15, 8, ALU.bitwise_and,
                                        ALU.bitwise_xor).then_inc(nib2_done, 1)
                dve.wait_ge(nib2_done, i + 1)
                nb = [nib2[:, a, 0:n * GROUP].rearrange("p (r c) -> p r c", c=GROUP) for a in range(2)]
                sc = s2s[:, 2 * r0:2 * r1].rearrange("p (r n) -> p n r", n=2)
                nc.vector.tensor_tensor(W2n[:, r0:r1, 0, :], nb[0], spread(sc[:, 0].unsqueeze(2), P, n, GROUP),
                                        ALU.mult)
                nc.vector.scalar_tensor_tensor(out=W2n[:, r0:r1, 1, :], in0=nb[1], scalar=-8.0,
                                               in1=spread(sc[:, 1].unsqueeze(2), P, n, GROUP),
                                               op0=ALU.add, op1=ALU.mult).then_inc(W2_done, 1)

            def w2_lo(t):
                rows = P if t < FT - 1 else FR
                dve.wait_ge(W2h_done, t + 1)
                perm = "h (p j) -> h j p"
                nc.vector.tensor_tensor(W2l[:, t, :].rearrange(perm, j=4)[0:rows],
                                        bank[6 + t % 2][0:rows, :].rearrange("h (j p) -> h j p", j=4),
                                        W2h[:, t, :].bitcast(f32).rearrange(perm, j=4)[0:rows],
                                        ALU.subtract).then_inc(ffn_read, 1)

            def ffn_add(u):
                for i in range(NT):
                    dve.wait_ge(ffn_ps, 8 * u + (i + 1))
                    if u:
                        dve.wait_ge(ffn_read, 8 * u + (FT + i - 7))
                    src = bank[6 + (FT + i) % 2][:, :]
                    if u:
                        nc.vector.tensor_tensor(gate[:, i, :], gate[:, i, :], src, ALU.add).then_inc(ffn_read, 1)
                    else:
                        nc.vector.tensor_copy(gate[:, i, :], src).then_inc(ffn_read, 1)

            dve.wait_ge(s13_in, 64)
            dve.wait_ge(zeroed, 4)
            dequant13(0, 0, 1)
            for i in range(4):
                x_lo(i)
            dequant13(1, 1, 1)
            for i in range(4, NT):
                x_lo(i)
            w13_lo(0, 0)
            w13_lo(1, 1)
            dve.wait_ge(s2_in, 16)
            for i in range(4):
                dequant2(i)
            hid(0)
            dequant13(2, 2, 1)
            for t in range(6):
                w2_lo(t)
            w13_lo(2, 0)
            hid(1)
            dequant13(3, 3, 1)
            for t in range(6, FT):
                w2_lo(t)
            for t in range(2, FT - 1):
                w13_lo(t + 1, (t + 1) % 2)
                if t + 2 < FT:
                    dequant13(t + 2, (t + 2) % 4, (t + 2) // 4 + 1)
                hid(t)
                if t % 2:
                    ffn_add(t // 2 - 1)
            hid(FT - 1)
            ffn_add(FT // 2 - 1)

            def cos_part(g, bp, c):
                dve.wait_ge(swapped, cnt(5, g, bp, c + 1))
                wait(dve, scores_ps, cnt(8, g, bp, -8))
                dst = q[:, bp, c - 1, :] if c else k[:, bp, :]
                nc.vector.tensor_tensor(dst.rearrange("p (b n) -> p b n", b=2),
                                        PJ_B[(c + 1 if c else 0) % 2][:, :].rearrange("p (b n) -> p b n", b=2),
                                        spread(cos.unsqueeze(1), P, 2, SEQ), ALU.mult).then_inc(cos_done, 1)

            def rotate(g, bp, c):
                dve.wait_ge(sin_done, cnt(5, g, bp, c + 1))
                dve.wait_ge(cos_done, cnt(5, g, bp, c + 1))
                dst = q[:, bp, c - 1, :] if c else k[:, bp, :]
                nc.vector.tensor_tensor(dst, dst, swap[:, (5 * bp + c) % 2, :], ALU.add).then_inc(rope_done, 1)

            def negate(g, bp, b, h):
                s = 4 * b + h
                dve.wait_ge(masked, cnt(8, g, bp, s + 1))
                nc.vector.tensor_scalar(nmx[:, s, :], mx[:, s, :], -SM, None, ALU.mult).then_inc(nmax_done, 1)

            def masking(g, bp, b, h0):
                wait(dve, pT_ps, cnt(6, g, bp, 3 * b - 3))
                for h in (h0, h0 + 1):
                    s = 4 * b + h
                    dve.wait_ge(scores_ps, cnt(8, g, bp, s + 1))
                    if h > h0:
                        negate(g, bp, b, h0)
                    else:
                        nc.vector.memset(pace[:, s // 2:s // 2 + 1], 0.0)
                    for i, (c0, c1) in enumerate(((0, P), (P, 3 * P))):
                        m = nc.vector.tensor_tensor_reduce(
                            out=probs[:, s, c0:c1], in0=S_B[s % 2][:, c0:c1], in1=mask[:, c0:c1], scale=1.0,
                            scalar=NEG, op0=ALU.add, op1=ALU.max, accum_out=mx[:, s, i:i + 1])
                    m.then_inc(masked, 1)
                negate(g, bp, b, h0 + 1)

            def normalise(g, bp, b, h):
                s = 4 * b + h
                dve.wait_ge(exp_done, cnt(8, g, bp, s + 1))
                nc.vector.reciprocal(rinv[:, s, :], rsum[:, s, :]).then_inc(rinv_done, 1)
                dve.wait_ge(rinv_done, cnt(8, g, bp, s + 1))
                for i, (c0, c1) in enumerate(((0, P), (P, 3 * P))):
                    m = nc.vector.tensor_scalar(probs[:, s, c0:c1], probs[:, s, c0:c1], rinv[:, s, i:i + 1], None,
                                                ALU.mult)
                m.then_inc(probs_done, 1)

            def p_lo(g, bp, b, r):
                dve.wait_ge(ph_done, cnt(6, g, bp, 3 * b + r + 1))
                nc.vector.tensor_tensor(pl[:, r, :], T_B[(7 * bp + 4 * b + r) % 2][:, :], ph[:, r, :].bitcast(f32),
                                        ALU.subtract).then_inc(pl_done, 1)

            def v_lo(g, bp, t_bank):
                dve.wait_ge(vh_done, cnt(1, g, bp, 1))
                nc.vector.tensor_tensor(vl[:, bp].rearrange("p t n -> p (t n)"), t_bank[:, :],
                                        vh[:, bp].rearrange("p t n -> p (t n)").bitcast(f32),
                                        ALU.subtract).then_inc(vl_done, 1)

            def o_lo(g, bp, j):
                dve.wait_ge(oh_done, cnt(4, g, bp, j + 1))
                nc.vector.tensor_tensor(ol[:, j].rearrange("p h n -> p (h n)"), O_B[j % 2][:, :],
                                        oh[:, j].rearrange("p h n -> p (h n)").bitcast(f32),
                                        ALU.subtract).then_inc(ol_done, 1)

            def accumulate(g, bp, t):
                dve.wait_ge(y_ps, cnt(4, g, bp, t + 1))
                wait(dve, acc_done, cnt(4, g, bp, t - 7))
                a, o = acc[:, 4 * bp + t, :], O_B[t % 2][:, :]
                if isinstance(g, int) and g == 0:
                    nc.vector.tensor_copy(a, o).then_inc(acc_done, 1)
                else:
                    nc.vector.tensor_tensor(a, a, o, ALU.add).then_inc(acc_done, 1)

            def finish(bp, t):
                n = 4 * bp + t
                dve.wait_ge(y_ps, cnt(4, NKV - 1, bp, t + 1))
                dve.wait_ge(rest_done, n + 1)
                o = gate[:, n, :]
                nc.vector.tensor_tensor(o, O_B[t % 2][:, :], o, ALU.mult).then_inc(acc_done, 1)
                dve.wait_ge(acc_done, 8 * (NKV - 1) + n + 1)
                nc.vector.tensor_tensor(o, o, acc[:, n, :], ALU.add).then_inc(final, 1)

            dve.wait_ge(hl_done, 2 * FT)
            cos_part(0, 0, 0)
            ffn_add(FT // 2)
            rotate(0, 0, 0)
            cos_part(0, 0, 1)
            v_lo(0, 0, T_B[1])
            rotate(0, 0, 1)
            for c in range(2, 5):
                cos_part(0, 0, c)
                rotate(0, 0, c)
            dve.wait_ge(const_in, 16)
            masking(0, 0, 0, 0)
            masking(0, 0, 0, 2)
            for h in range(GH):
                normalise(0, 0, 0, h)

            def step(g, bp, last):
                ng, nbp = (g, 1) if bp == 0 else (g + 1, 0)
                more = not (last and bp == 1)
                if not more:
                    p_lo(g, bp, 0, 0)
                    p_lo(g, bp, 0, 1)
                    finish(0, 3)
                    p_lo(g, bp, 0, 2)
                    o_lo(g, bp, 0)
                    o_lo(g, bp, 1)
                    p_lo(g, bp, 1, 0)
                    p_lo(g, bp, 1, 1)
                    finish(1, 0)
                    p_lo(g, bp, 1, 2)
                    finish(1, 1)
                    o_lo(g, bp, 2)
                    o_lo(g, bp, 3)
                    finish(1, 2)
                    finish(1, 3)
                    return
                for r in range(3):
                    p_lo(g, bp, 0, r)
                if more:
                    cos_part(ng, nbp, 0)
                o_lo(g, bp, 0)
                o_lo(g, bp, 1)
                if more:
                    rotate(ng, nbp, 0)
                masking(g, bp, 1, 0)
                normalise(g, bp, 1, 0)
                normalise(g, bp, 1, 1)
                masking(g, bp, 1, 2)
                if more:
                    cos_part(ng, nbp, 1)
                normalise(g, bp, 1, 2)
                normalise(g, bp, 1, 3)
                if more:
                    v_lo(ng, nbp, T_B[(7 * bp + 3) % 2])
                    rotate(ng, nbp, 1)
                    cos_part(ng, nbp, 2)
                    rotate(ng, nbp, 2)
                    cos_part(ng, nbp, 3)
                p_lo(g, bp, 1, 0)
                p_lo(g, bp, 1, 1)
                p_lo(g, bp, 1, 2)
                if more:
                    rotate(ng, nbp, 3)
                if more:
                    cos_part(ng, nbp, 4)
                o_lo(g, bp, 2)
                o_lo(g, bp, 3)
                masking(ng, nbp, 0, 0)
                rotate(ng, nbp, 4)
                if last:
                    finish(0, 0)
                    masking(ng, nbp, 0, 2)
                    normalise(ng, nbp, 0, 0)
                    normalise(ng, nbp, 0, 1)
                    finish(0, 1)
                    masking(ng, nbp, 1, 0)
                    normalise(ng, nbp, 0, 2)
                    normalise(ng, nbp, 0, 3)
                    masking(ng, nbp, 1, 2)
                    finish(0, 2)
                    for h in range(GH):
                        normalise(ng, nbp, 1, h)
                    return
                accumulate(g, bp, 0)
                masking(ng, nbp, 0, 2)
                normalise(ng, nbp, 0, 0)
                normalise(ng, nbp, 0, 1)
                accumulate(g, bp, 1)
                normalise(ng, nbp, 0, 2)
                normalise(ng, nbp, 0, 3)
                accumulate(g, bp, 2)
                accumulate(g, bp, 3)

            def group(g, last=False):
                step(g, 0, last)
                step(g, 1, last)

            group(0)
            with dve.Fori(1, NKV - 1) as g:
                group(g)
            group(NKV - 1, True)

        @block.tensor
        def _(pe):
            def three(out_, pairs, midway=None):
                n = len(pairs)
                for i, (sh, sl, mh, ml) in enumerate(pairs):
                    if midway and i == n // 2:
                        midway()
                    nc.tensor.matmul(out_, sh, mh, start=(i == 0), stop=False)
                    nc.tensor.matmul(out_, sh, ml, start=False, stop=False)
                    m = nc.tensor.matmul(out_, sl, mh, start=False, stop=(i == n - 1))
                return m

            pe.wait_ge(const_in, 16)
            for i in range(NT):
                pe.wait_ge(xn_done, i + 1)
                wait(pe, xl_done, i - 3)
                for d in range(DT):
                    m = nc.tensor.transpose(bank[i % 4][:, d * P:(d + 1) * P], xn[:, i, d * P:(d + 1) * P], ident)
                m.then_inc(xT_ps, 1)

            def w13_turn(t, s2_):
                pe.wait_ge(W13_done, t + 1)
                for m in range(2):
                    wait(pe, W13l_done, 2 * t + (m - 1))
                    for d in range(DT):
                        i = nc.tensor.transpose(bank[m][:, d * P:(d + 1) * P],
                                                W13[:, s2_, m, d * P:(d + 1) * P], ident)
                    i.then_inc(W13_ps, 1)

            def w13_mult(t, s2_):
                for half in range(2):
                    wait(pe, h_done, 2 * t + (half - 1))
                    cols = slice(half * IT, half * IT + IT)
                    for m in range(2):
                        pe.wait_ge(W13l_done, 2 * t + (m + 1))
                        three(bank[2 + 2 * half + m][:, :],
                              [(W13h[:, s2_, m, d, :], W13l[:, s2_, m, d, :], xh[:, d, cols], xl[:, d, cols])
                               for d in range(DT)]).then_inc(ab_ps, 1)

            def w2_turn(t):
                rows = P if t < FT - 1 else FR
                wait(pe, ffn_read, t - 1)
                W2f = W2n[:, :, :, :].rearrange("p r n c -> p (r n c)")
                for j in range(4):
                    i = nc.tensor.transpose(bank[6 + t % 2][0:rows, j * P:(j + 1) * P],
                                            W2f[:, j * F + t * P:j * F + t * P + rows], ident)
                i.then_inc(W2_ps, 1)

            def w2_mult(u, pair):
                for i in range(NT):
                    if i == 0:
                        pe.wait_ge(hl_done, 4 * u + 2 * len(pair))
                    wait(pe, ffn_read, 8 * u + (FT + i - 1))
                    cols = slice(i * P, (i + 1) * P)
                    three(bank[6 + (FT + i) % 2][:, :],
                          [(hh[s][:, cols], hl[s][:, cols],
                            W2h[:, bass.ds(2 * u + e, 1), :].rearrange("p o d -> p (o d)"),
                            W2l[:, bass.ds(2 * u + e, 1), :].rearrange("p o d -> p (o d)"))
                           for e, s in enumerate(pair)]).then_inc(ffn_ps, 1)

            pe.wait_ge(xl_done, NT)
            w13_turn(0, 0)
            w13_turn(1, 1)
            w13_mult(0, 0)
            pe.wait_ge(W2_done, 4)
            for t in range(6):
                w2_turn(t)
            w13_turn(2, 0)
            w13_mult(1, 1)
            for t in range(6, FT):
                w2_turn(t)
            with pe.Fori(0, 2) as v:
                for j in range(4):
                    w13_turn(4 * v + (3 + j), (3 + j) % 2)
                    w13_mult(4 * v + (2 + j), (2 + j) % 2)
                    if j % 2:
                        w2_mult(2 * v + j // 2, (0, 1) if j == 1 else (2, 3))
            w13_mult(FT - 1, (FT - 1) % 2)
            w2_mult(FT // 2 - 1, (0, 1))

            def project(g, bp, c, midway=None):
                if bp == 0:
                    pe.wait_ge(wl_done, in_chunk(g, c) + 1)
                if c == 3:
                    wait(pe, vT_done, cnt(1, g, bp, 1))
                else:
                    r = {0: -1, 1: 0, 2: 1, 4: 2, 5: 3}[c]
                    wait(pe, cos_done, cnt(5, g, bp, r))
                cols = slice(bp * IT, bp * IT + IT)
                three(PJ_B[c % 2][:, :],
                      [(wih[:, c, d, :], wil[:, c, d, :], xh[:, d, cols], xl[:, d, cols])
                       for d in range(DT)], midway).then_inc(proj_ps, 1)

            def v_turn(g, bp, t_bank):
                pe.wait_ge(vT_done, cnt(1, g, bp, 1))
                for t in range(IT // P):
                    i = nc.tensor.transpose(t_bank[:, t * P:(t + 1) * P], vT[:, t * P:(t + 1) * P], ident)
                i.then_inc(v_ps, 1)

            def scores(g, bp, b, h):
                s = 4 * b + h
                if b == 0:
                    pe.wait_ge(rope_done, cnt(5, g, bp, h + 2))
                wait(pe, masked, cnt(8, g, bp, s - 1))
                c = b * SEQ
                nc.tensor.matmul(S_B[s % 2][:, 0:P], q[:, bp, h, c:c + P], k[:, bp, c:c + P], start=True, stop=True)
                nc.tensor.matmul(S_B[s % 2][:, P:3 * P], q[:, bp, h, c + P:c + SEQ], k[:, bp, c:c + SEQ],
                                 start=True, stop=True).then_inc(scores_ps, 1)

            def p_turn(g, bp, b, r, last):
                j = 4 * b + r
                if r == 0:
                    pe.wait_ge(probs_done, cnt(8, g, bp, 4 * b + 4))
                if j == 5:
                    if last:
                        pe.wait_ge(pl_done, cnt(6, g, bp, 2))
                    else:
                        pe.wait_ge(vl_done, cnt(1, g, bp, 2))
                else:
                    wait(pe, pl_done, cnt(6, g, bp, {0: -1, 1: 0, 2: 1, 4: 3, 6: 4}[j]))
                    if j == 1:
                        pe.wait_ge(vl_done, cnt(1, g, bp, 1))
                for h in range(GH):
                    i = nc.tensor.transpose(T_B[(7 * bp + j) % 2][:, h * P:(h + 1) * P],
                                            probs[:, 4 * b + h, r * P:(r + 1) * P], ident)
                i.then_inc(pT_ps, 1)

            def attend(g, bp, b, late=False):
                pe.wait_ge(vl_done, cnt(1, g, bp, 1))
                for t in range(2):
                    j = 2 * b + t
                    if b == 0:
                        wait(pe, acc_done, cnt(4, g, bp, t - 1))
                    else:
                        pe.wait_ge(ol_done, cnt(4, g, bp, t + 1))
                    if late:
                        pe.wait_ge(acc_done, cnt(4, g, bp, t + 1))
                    blocks = ((0, 0),) if t == 0 else ((1, 0), (2, 1))
                    pe.wait_ge(pl_done, cnt(6, g, bp, 3 * b + (1 if t == 0 else 3)))
                    three(O_B[j % 2][:, :], [(vh[:, bp, 2 * b + kt, :], vl[:, bp, 2 * b + kt, :],
                                              ph[:, r, :], pl[:, r, :]) for r, kt in blocks]).then_inc(o_ps, 1)

            def out_project(g, bp, t, early=False):
                pe.wait_ge(ol_done, cnt(4, g, bp, t + 1 if t > 1 or early else t + 3))
                if t > 1:
                    pe.wait_ge(acc_done, cnt(4, g, bp, t - 1))
                if bp == 0 and t == 0:
                    pe.wait_ge(wl_done, wo_chunk(g, GH - 1) + 1)
                three(O_B[t % 2][:, :], [(oh[:, t, h, :], ol[:, t, h, :], woh[:, h, :], wol[:, h, :])
                                         for h in range(GH)]).then_inc(y_ps, 1)

            pe.wait_ge(h_done, 2 * FT)
            project(0, 0, 0)
            project(0, 0, 1)
            w2_mult(FT // 2, (2,))
            project(0, 0, 2)
            v_turn(0, 0, T_B[1])
            for c in range(3, 6):
                project(0, 0, c)
            for h in range(GH):
                scores(0, 0, 0, h)

            def step(g, bp, last):
                ng, nbp = (g, 1) if bp == 0 else (g + 1, 0)
                more = not (last and bp == 1)
                if not more:
                    p_turn(g, bp, 0, 0, True)
                    p_turn(g, bp, 0, 1, True)
                    out_project(g, 0, 3)
                    p_turn(g, bp, 0, 2, True)
                    attend(g, bp, 0)
                    p_turn(g, bp, 1, 0, True)
                    p_turn(g, bp, 1, 1, True)
                    out_project(g, bp, 0, True)
                    p_turn(g, bp, 1, 2, True)
                    out_project(g, bp, 1, True)
                    attend(g, bp, 1, True)
                    out_project(g, bp, 2)
                    out_project(g, bp, 3)
                    return
                p_turn(g, bp, 0, 0, not more)
                p_turn(g, bp, 0, 1, not more)
                if more:
                    project(ng, nbp, 0)
                p_turn(g, bp, 0, 2, not more)
                if more:
                    project(ng, nbp, 1)
                attend(g, bp, 0)
                scores(g, bp, 1, 0)
                scores(g, bp, 1, 1)
                if more:
                    project(ng, nbp, 2)
                scores(g, bp, 1, 2)
                scores(g, bp, 1, 3)
                if more:
                    pe.wait_ge(pl_done, cnt(6, g, bp, 2))
                    v_turn(ng, nbp, T_B[(7 * bp + 3) % 2])
                    project(ng, nbp, 3)
                    project(ng, nbp, 4)
                p_turn(g, bp, 1, 0, not more)
                p_turn(g, bp, 1, 1, not more)
                if more:
                    project(ng, nbp, 5, lambda: p_turn(g, bp, 1, 2, False))
                attend(g, bp, 1)
                if more:
                    scores(ng, nbp, 0, 0)
                    scores(ng, nbp, 0, 1)
                out_project(g, bp, 0)
                scores(ng, nbp, 0, 2)
                scores(ng, nbp, 0, 3)
                out_project(g, bp, 1)
                if last:
                    scores(ng, nbp, 1, 0)
                    scores(ng, nbp, 1, 1)
                    out_project(g, bp, 2)
                    scores(ng, nbp, 1, 2)
                    scores(ng, nbp, 1, 3)
                    return
                out_project(g, bp, 2)
                out_project(g, bp, 3)

            def group(g, last=False):
                step(g, 0, last)
                step(g, 1, last)

            group(0)
            with pe.Fori(1, NKV - 1) as g:
                group(g)
            group(NKV - 1, True)


def constants():
    inv = (np.float32(10000.0) ** (-np.arange(HALF, dtype=np.float32) / np.float32(HALF))).astype(np.float32)
    ang = np.arange(SEQ, dtype=np.float32)[None, :] * inv[:, None]
    cos, sin = np.cos(ang), np.sin(ang)
    c = np.zeros((P, C_W), np.float32)
    c[:, C_COS:C_COS + SEQ] = np.concatenate([cos, cos])
    c[:, C_SIN:C_SIN + SEQ] = np.concatenate([-sin, sin])
    i, j = np.arange(P)[:, None], np.arange(P)[None, :]
    for n, ok in enumerate((j <= i, j > i, j <= i)):
        c[:, C_MASK + n * P:C_MASK + (n + 1) * P] = np.where(ok, 0.0, NEG)
    c[:, C_ID:C_ID + P] = np.eye(P)
    return c


_INS = ["L0_attn_x", "L0_attn_wq", "L0_attn_wk", "L0_attn_wv", "L0_attn_wo",
        "L0_ffn_w1", "L0_ffn_s1", "L0_ffn_w2", "L0_ffn_s2", "L0_ffn_w3", "L0_ffn_s3"]


def kernel(**inputs):
    import numpy as _np
    import concourse.bacc as _bacc
    from concourse import mybir as _mybir
    from concourse.bass_utils import run_bass_kernel_spmd as _run

    nc = _bacc.Bacc("TRN2", target_bir_lowering=False, num_devices=1)
    arrays, args = {}, []
    for name, a in [(n, inputs[n]) for n in _INS] + [("constants", constants())]:
        a = _np.ascontiguousarray(a)
        arrays[f"in_{name}"] = a
        args.append(nc.dram_tensor(f"in_{name}", a.shape, _mybir.dt.from_np(a.dtype), kind="ExternalInput").ap())
    args.append(nc.dram_tensor("out_0", (B, SEQ, D), _mybir.dt.float32, kind="ExternalOutput").ap())
    build(nc, *args)
    r = _run(nc, [arrays], core_ids=[0])
    return r.results[0]["out_0"]
```

```python
from contextlib import ExitStack

import numpy as np
import concourse.bass as bass
from concourse import mybir

B, SEQ, D = 4, 256, 512
HD, NQ, NKV = 128, 32, 8
GH = NQ // NKV
HALF = HD // 2
F = 1376
GROUP = 64
P = 128
TOK = B * SEQ
NT = TOK // P
DT = D // P
IT = 512
FT = -(-F // P)
FR = F - (FT - 1) * P
PK = D // 2
R2 = F * D // 2 // GROUP // P
EPS = 1e-5
SM = float(HD) ** -0.5
NEG = -3.0e38
RING = 5
CHUNKS = 6 + GH
ALL_W = CHUNKS * NKV
ALL_Y = NT * NKV
C_COS, C_SIN, C_MASK, C_ID, C_W = 0, SEQ, 2 * SEQ, 2 * SEQ + 3 * P, 2 * SEQ + 4 * P


def build(nc, x, wq, wk, wv, wo, w1, s1, w2, s2, w3, s3, const, out):
    f32, f32r, i32 = mybir.dt.float32, mybir.dt.float32r, mybir.dt.int32
    ALU, ACT = mybir.AluOpType, mybir.ActivationFunctionType

    x_v = x.rearrange("b (t p) d -> p (b t) d", p=P)
    out_v = out.rearrange("b (t p) d -> p (b t) d", p=P)
    wq_v = wq.rearrange("(t p) n -> p t n", p=P)
    wk_v = wk.rearrange("(t p) n -> p t n", p=P)
    wv_v = wv.rearrange("(t p) n -> p t n", p=P)
    w13_v = [w.rearrange("(h r) c -> h (r c)", r=PK // GROUP) for w in (w1, w3)]
    s13_v = [s.rearrange("(h g) -> h g", g=D // GROUP) for s in (s1, s3)]
    w2_v = w2.rearrange("(p r) c -> p (r c)", r=R2)
    s2_v = s2.rearrange("(p g) -> p g", g=2 * R2)

    ctx = ExitStack()
    with ctx:
        def sb(name, shape, dt, at=ctx):
            return at.enter_context(nc.sbuf_tensor(name, shape, dt))

        def sem(name):
            return ctx.enter_context(nc.semaphore(name))

        gate = sb("gate", [P, NT, D], f32)
        cst = sb("cst", [P, C_W], f32)
        cos, sin = cst[:, C_COS:C_COS + SEQ], cst[:, C_SIN:C_SIN + SEQ]
        mask, ident = cst[:, C_MASK:C_MASK + 3 * P], cst[:, C_ID:C_ID + P]
        raw = sb("raw", [P, RING, D], f32)
        xh = sb("xh", [P, DT, TOK], f32r)
        xl = sb("xl", [P, DT, TOK], f32r)
        main = ctx.enter_context(ExitStack())

        ffn = ctx.enter_context(ExitStack())
        packed = sb("packed", [P, 2, 2, PK], i32, ffn)
        s13 = sb("s13", [P, FT, 2, D // GROUP], f32, ffn)
        nib = sb("nib", [P, 2, 2 * PK], i32, ffn)
        W13 = sb("W13", [P, 2, 2, D], f32, ffn)
        W13h = sb("W13h", [P, 2, 2, DT, P], f32r, ffn)
        W13l = sb("W13l", [P, 2, 2, DT, P], f32r, ffn)
        NR2 = 11
        packed2 = sb("packed2", [P, 2, NR2 * GROUP], i32, ffn)
        nib2 = sb("nib2", [P, 2, NR2 * GROUP], i32, ffn)
        s2s = sb("s2s", [P, 2 * R2], f32, ffn)
        stat = sb("stat", [P, NT, 6], f32, ffn)
        mv = sb("mv", [P, NT, 2], f32, ffn)
        std = sb("std", [P, 4, NT], f32, ffn)
        act_h = sb("act_h", [P, 2, IT], f32, ffn)
        early = ffn.enter_context(ExitStack())
        W2n = sb("W2n", [P, R2, 2, GROUP], f32, early)
        xn = sb("xn", [P, NT, D], f32, early)
        early.close()
        sb("over_W2n", [P, R2, 2, GROUP], f32, ffn)
        hh = sb("hh", [P, 2, TOK], f32r, ffn)
        hl = sb("hl", [P, 2, TOK], f32r, ffn)
        W2raw = sb("W2raw", [P, 2, D], f32, ffn)
        W2h = sb("W2h", [P, FT, D], f32r, ffn)
        W2l = sb("W2l", [P, FT, D], f32r, ffn)
        ffn.close()

        wih = sb("wih", [P, 6, DT, P], f32r, main)
        wil = sb("wil", [P, 6, DT, P], f32r, main)
        swap = sb("swap", [P, 2, IT], f32, main)
        vT = sb("vT", [P, IT], f32, main)
        k = sb("k", [P, 2, IT], f32, main)
        kh = sb("kh", [P, 2, IT], f32r, main)
        kl = sb("kl", [P, 2, IT], f32r, main)
        q = sb("q", [P, GH, IT], f32, main)
        qh = sb("qh", [P, GH, 2, P], f32r, main)
        ql = sb("ql", [P, GH, 2, P], f32r, main)
        probs = sb("probs", [P, 2 * GH, 3 * P], f32, main)
        vh = sb("vh", [P, 2, IT // P, HD], f32r, main)
        vl = sb("vl", [P, 2, IT // P, HD], f32r, main)
        mx = sb("mx", [P, 2 * GH, 2], f32, main)
        pace = sb("pace", [P, 4], f32, main)
        nmx = sb("nmx", [P, 2 * GH, 2], f32, main)
        rsum = sb("rsum", [P, 2 * GH, 2], f32, main)
        rinv = sb("rinv", [P, 2 * GH, 2], f32, main)
        ph = sb("ph", [P, 3, GH * P], f32r, main)
        pl = sb("pl", [P, 3, GH * P], f32r, main)
        oh = sb("oh", [P, 4, GH, P], f32r, main)
        ol = sb("ol", [P, 4, GH, P], f32r, main)
        woh = sb("woh", [P, GH, D], f32r, main)
        wol = sb("wol", [P, GH, D], f32r, main)
        acc = sb("acc", [P, NT, D], f32, main)

        bank = [ctx.enter_context(nc.psum_tensor(f"bank{i}", [P, 512], f32)) for i in range(8)]
        S_B, PJ_B, T_B, O_B = bank[0:2], bank[2:4], bank[4:6], bank[6:8]
        X_B = (2, 3, 4, 5, 4, 5, 6, 7)

        const_in, s13_in, s2_in, out_done = sem("const_in"), sem("s13_in"), sem("s2_in"), sem("out_done")
        x_in = [sem(f"x_in{i}") for i in range(NT)]
        w13_in = [sem(f"w13_in{i}") for i in range(2)]
        w2_in = [sem(f"w2_in{i}") for i in range(2)]
        raw_in = [sem(f"raw_in{i}") for i in range(RING)]
        zeroed, stats_done, mv_done, ln_small, std_done = (
            sem("zeroed"), sem("stats_done"), sem("mv_done"), sem("ln_small"), sem("std_done"))
        xn_done, xT_ps, xh_done, xl_done = sem("xn_done"), sem("xT_ps"), sem("xh_done"), sem("xl_done")
        nib_done, W13_done, W13_ps, W13h_done, W13l_done = (
            sem("nib_done"), sem("W13_done"), sem("W13_ps"), sem("W13h_done"), sem("W13l_done"))
        nib2_done, W2_done, W2_ps, W2h_done, W2l_done = (
            sem("nib2_done"), sem("W2_done"), sem("W2_ps"), sem("W2h_done"), sem("W2l_done"))
        ab_ps, silu_done, h_done, hh_done, hl_done = (
            sem("ab_ps"), sem("silu_done"), sem("h_done"), sem("hh_done"), sem("hl_done"))
        ffn_ps, ffn_read, gate_done = sem("ffn_ps"), sem("ffn_read"), sem("gate_done")
        scores_ps, masked, nmax_done, exp_done, rinv_done, probs_done = (
            sem("scores_ps"), sem("masked"), sem("nmax_done"), sem("exp_done"), sem("rinv_done"),
            sem("probs_done"))
        proj_ps, cos_done, swapped, sin_done, rope_done = (
            sem("proj_ps"), sem("cos_done"), sem("swapped"), sem("sin_done"), sem("rope_done"))
        kqh_done, kql_done = sem("kqh_done"), sem("kql_done")
        vT_done, v_ps, vh_done, vl_done = sem("vT_done"), sem("v_ps"), sem("vh_done"), sem("vl_done")
        pT_ps, ph_done, pl_done = sem("pT_ps"), sem("ph_done"), sem("pl_done")
        o_ps, oh_done, ol_done = sem("o_ps"), sem("oh_done"), sem("ol_done")
        y_ps, acc_done = sem("y_ps"), sem("acc_done")
        wh_done, wl_done = sem("wh_done"), sem("wl_done")
        rest_mul, rest_done = sem("rest_mul"), sem("rest_done")
        final, last_final = sem("final"), sem("last_final")

        def wait(eng, s, value):
            if isinstance(value, int) and value <= 0:
                return
            eng.wait_ge(s, value)

        def cnt(per, g, bp, c):
            return 2 * per * g + (per * bp + c)

        def second(ap):
            return ap.rearrange("p (b t n) -> p b t n", b=2, t=2)[:, :, 1, :]

        def spread(ap, *sizes):
            return ap.to_broadcast(list(sizes))

        block = ctx.enter_context(nc.Block())

        def wo_chunk(g, h):
            return CHUNKS * g + (6 + h)

        def in_chunk(g, c):
            return CHUNKS * g + c

        @block.sync
        def _(sp):
            def load_x(i):
                sp.dma_start(xn[:, i, :], x_v[:, i, :]).then_inc(x_in[i], 16)

            for i in range(4):
                load_x(i)
            sp.dma_start(cst[:, :], const).then_inc(const_in, 16)

            def load13(t):
                rows = P if t < FT - 1 else FR
                wait(sp, nib_done, t - 1)
                for m in range(2):
                    sp.dma_start(packed[0:rows, t % 2, m, :], w13_v[m][t * P:t * P + rows, :]) \
                        .then_inc(w13_in[t % 2], 16)

            load13(0)
            sp.wait_ge(zeroed, 1)
            for m in range(2):
                sp.dma_start(s13[:, 0:FT - 1, m, :],
                             s13_v[m][0:(FT - 1) * P, :].rearrange("(t p) g -> p t g", p=P)).then_inc(s13_in, 16)
                sp.dma_start(s13[0:FR, FT - 1, m, :], s13_v[m][(FT - 1) * P:F, :]).then_inc(s13_in, 16)
            for i in range(4, NT):
                load_x(i)
            load13(1)
            sp.dma_start(s2s[:, :], s2_v).then_inc(s2_in, 16)
            for i in range(4):
                r0, r1 = NR2 * i, min(NR2 * i + NR2, R2)
                wait(sp, nib2_done, i - 1)
                sp.dma_start(packed2[:, i % 2, 0:(r1 - r0) * GROUP],
                             w2_v[:, r0 * GROUP:r1 * GROUP]).then_inc(w2_in[i % 2], 16)
                if i == 1:
                    load13(2)
                    load13(3)
            for t in range(4, FT):
                load13(t)

            def load_in(w, g, c):
                src = (wk_v, wv_v)[c][:, :, bass.ds(g * HD, HD)] if c < 2 else \
                    wq_v[:, :, bass.ds(g * (GH * HD) + (c - 2) * HD, HD)]
                s = w if isinstance(w, int) else c + CHUNKS
                sp.dma_start(raw[:, s % RING, :].rearrange("p (t n) -> p t n", t=DT), src) \
                    .then_inc(raw_in[s % RING], 16)

            for c in range(6):
                wait(sp, wl_done, c - RING + 1)
                load_in(c, 0, c)

            def group_loads(g, last):
                for h in range(GH):
                    wait(sp, wl_done, wo_chunk(g, h) - RING + 1)
                    sp.dma_start(raw[:, (6 + h) % RING, :], wo[bass.ds(g * (GH * HD) + h * HD, HD), :]) \
                        .then_inc(raw_in[(6 + h) % RING], 16)
                if not last:
                    for c in range(6):
                        wait(sp, wl_done, in_chunk(g + 1, c) - RING + 1)
                        load_in(None, g + 1, c)

            group_loads(0, False)
            with sp.Fori(1, NKV - 1) as g:
                group_loads(g, False)
            group_loads(NKV - 1, True)
            for t in range(NT + RING):
                if t < NT:
                    if t < RING:
                        sp.wait_ge(wl_done, ALL_W + t - RING + 1)
                    else:
                        sp.wait_ge(rest_done, t - RING + 1)
                    sp.dma_start(raw[:, (ALL_W + t) % RING, :], x_v[:, t, :]).then_inc(raw_in[(ALL_W + t) % RING], 16)
                if t >= RING:
                    if t - RING < NT - 1:
                        sp.wait_ge(final, t - RING + 1)
                    else:
                        sp.wait_ge(last_final, 1)
                    sp.dma_start(out_v[:, t - RING, :], gate[:, t - RING, :]).then_inc(out_done, 16)
            sp.wait_ge(out_done, 16 * NT)

        @block.gpsimd
        def _(pool):
            nc.gpsimd.memset(s13[:, FT - 1, :, :], 0.0).then_inc(zeroed, 1)
            pool.wait_ge(zeroed, 1)
            nc.gpsimd.memset(W2h[FR:P, FT - 1, :].bitcast(f32), 0.0).then_inc(zeroed, 1)
            pool.wait_ge(zeroed, 2)
            nc.gpsimd.memset(W2l[FR:P, FT - 1, :].bitcast(f32), 0.0).then_inc(zeroed, 1)

            def hid_lo(t, s):
                for half in range(2):
                    pool.wait_ge(hh_done, 2 * t + (half + 1))
                    cols = slice(half * IT, half * IT + IT)
                    nc.gpsimd.tensor_tensor(hl[:, s, cols], act_h[:, half, :], hh[:, s, cols].bitcast(f32),
                                            ALU.subtract).then_inc(hl_done, 1)

            hid_lo(0, 0)
            hid_lo(1, 1)
            for t in range(FT):
                rows = P if t < FT - 1 else FR
                pool.wait_ge(W2h_done, t + 1)
                nc.gpsimd.tensor_tensor(W2l[0:rows, t, :], W2raw[0:rows, t % 2, :],
                                        W2h[0:rows, t, :].bitcast(f32), ALU.subtract).then_inc(W2l_done, 1)
            hid_lo(2, 0)
            with pool.Fori(0, 3) as v:
                hid_lo(2 * v + 3, 1)
                hid_lo(2 * v + 4, 0)
            hid_lo(9, 1)

            def w_lo(w, slot, hi, lo):
                pool.wait_ge(wh_done, w + 1)
                nc.gpsimd.tensor_tensor(lo, raw[:, slot, :], hi.bitcast(f32), ALU.subtract).then_inc(wl_done, 1)

            def flat(ap):
                return ap.rearrange("p t n -> p (t n)")

            def lo_in(g, c):
                w_lo(in_chunk(g, c), c % RING, flat(wih[:, c]), flat(wil[:, c]))

            def lo_wo(g, h):
                w_lo(wo_chunk(g, h), (6 + h) % RING, woh[:, h, :], wol[:, h, :])

            def sin_part(g, bp, c):
                s = (5 * bp + c) % 2
                pool.wait_ge(swapped, cnt(5, g, bp, c + 1))
                v = swap[:, s, :].rearrange("p (b n) -> p b n", b=2)
                nc.gpsimd.tensor_tensor(v, v, spread(sin.unsqueeze(1), P, 2, SEQ), ALU.mult).then_inc(sin_done, 1)

            pool.wait_ge(ab_ps, 4 * FT)
            for c in range(6):
                lo_in(0, c)
            hid_lo(10, 0)
            for c in range(5):
                sin_part(0, 0, c)

            def rest(t):
                pool.wait_ge(acc_done, 8 * (NKV - 2) + t + 1)
                pool.wait_ge(gate_done, NT)
                nc.gpsimd.tensor_tensor(acc[:, t, :], acc[:, t, :], gate[:, t, :], ALU.mult).then_inc(rest_mul, 1)
                w = ALL_W + t
                pool.wait_ge(rest_mul, t + 1)
                pool.wait_ge(raw_in[w % RING], 16 * (w // RING + 1))
                nc.gpsimd.tensor_tensor(acc[:, t, :], acc[:, t, :], raw[:, w % RING, :], ALU.add) \
                    .then_inc(rest_done, 1)

            def add_rest(t):
                pool.wait_ge(acc_done, 8 * (NKV - 1) + t + 1)
                nc.gpsimd.tensor_tensor(gate[:, t, :], gate[:, t, :], acc[:, t, :], ALU.add).then_inc(final, 1)

            def step(g, bp, last):
                ng, nbp = (g, 1) if bp == 0 else (g + 1, 0)
                w = bp == 0
                nxt = w and not last
                if last and bp == 1:
                    for t in range(4, NT):
                        rest(t)
                        add_rest(t - 4)
                    for t in range(4, NT - 1):
                        add_rest(t)
                    return
                sin_part(ng, nbp, 0)
                if w:
                    for h in range(GH):
                        lo_wo(g, h)
                for c in range(1, 5):
                    sin_part(ng, nbp, c)
                    if w and last:
                        rest(c - 1)
                if nxt:
                    for c in range(6):
                        lo_in(g + 1, c)

            def group(g, last=False):
                step(g, 0, last)
                step(g, 1, last)

            group(0)
            with pool.Fori(1, NKV - 1) as g:
                group(g)
            group(NKV - 1, True)

        @block.scalar
        def _(act):
            def root(part):
                act.wait_ge(ln_small, 6 * part + 1)
                cols = slice(4 * part, 4 * part + 4)
                nc.scalar.activation(std[:, 1, cols], std[:, 0, cols], ACT.Sqrt).then_inc(std_done, 1)

            def x_hi(tiles):
                for i in tiles:
                    act.wait_ge(xT_ps, i + 1)
                    nc.scalar.activation(xh[:, :, i * P:(i + 1) * P],
                                         bank[X_B[i]][:, :].rearrange("p (t n) -> p t n", t=DT),
                                         ACT.Copy).then_inc(xh_done, 1)

            def w13_hi(t, s):
                for m in range(2):
                    act.wait_ge(W13_ps, 2 * t + (m + 1))
                    wait(act, ab_ps, 4 * t - 4)
                    nc.scalar.activation(W13h[:, s, m].rearrange("p t n -> p (t n)"), bank[m][:, :],
                                         ACT.Copy).then_inc(W13h_done, 1)

            def silu(t, half):
                act.wait_ge(ab_ps, 4 * t + (2 * half + 1))
                wait(act, hl_done, 2 * t + (half - 1))
                nc.scalar.activation(act_h[:, half, :], bank[2 + 2 * half][:, :], ACT.Silu).then_inc(silu_done, 1)

            def hid_hi(t, u, s, half):
                act.wait_ge(h_done, 2 * t + (half + 1))
                wait(act, ffn_read, 8 * u)
                nc.scalar.activation(hh[:, s, half * IT:half * IT + IT],
                                     act_h[:, half, :], ACT.Copy).then_inc(hh_done, 1)

            def hidden(t, u, s):
                silu(t, 0)
                hid_hi(t, u, s, 0)
                silu(t, 1)
                w13_hi(t + 1, 1 - s)
                hid_hi(t, u, s, 1)

            def w2_split(tiles):
                for t in tiles:
                    rows = P if t < FT - 1 else FR
                    act.wait_ge(W2_ps, t + 1)
                    wait(act, W2l_done, t - 1)
                    src = bank[6 + t % 2][0:rows, :].rearrange("h (j p) -> h j p", j=4)
                    nc.scalar.activation(W2raw[0:rows, t % 2, :].rearrange("h (p j) -> h j p", j=4), src, ACT.Copy)
                    nc.scalar.activation(W2h[0:rows, t, :].rearrange("h (p j) -> h j p", j=4), src,
                                         ACT.Copy).then_inc(W2h_done, 1)

            root(0)
            act.wait_ge(zeroed, 3)
            x_hi(range(4))
            w13_hi(0, 0)
            root(1)
            x_hi(range(4, NT))
            silu(0, 0)
            hid_hi(0, 0, 0, 0)
            silu(0, 1)
            w13_hi(1, 1)
            hid_hi(0, 0, 0, 1)
            hidden(1, 0, 1)
            silu(2, 0)
            w2_split(range(4))
            silu(2, 1)
            w2_split(range(4, 6))
            w13_hi(3, 1)
            w2_split(range(6, FT))
            hid_hi(2, 1, 0, 0)
            hid_hi(2, 1, 0, 1)
            hidden(3, 1, 1)
            hidden(4, 2, 0)
            with act.Fori(1, 3) as v:
                hidden(2 * v + 3, v + 1, 1)
                hidden(2 * v + 4, v + 2, 0)
            hidden(9, 4, 1)
            silu(10, 0)
            silu(10, 1)

            def w_hi(slot, use, hi):
                act.wait_ge(raw_in[slot], 16 * use)
                nc.scalar.activation(hi, raw[:, slot, :], ACT.Copy).then_inc(wh_done, 1)

            def hi_in(g, c):
                wait(act, proj_ps, cnt(6, g, -1, c + 1))
                w_hi(c % RING, 2 * g + (c // RING + 1), wih[:, c].rearrange("p t n -> p (t n)"))

            def hi_wo(g, h):
                wait(act, y_ps, 8 * g)
                w_hi((6 + h) % RING, 2 * g + ((6 + h) // RING + 1), woh[:, h, :])

            def halves(g, bp, c):
                a = 5 * bp + c
                act.wait_ge(proj_ps, cnt(6, g, bp, (c + 2 if c else 1)))
                wait(act, rope_done, cnt(5, g, bp, c - 1))
                src = PJ_B[(c + 1 if c else 0) % 2]
                nc.scalar.activation(swap[0:HALF, a % 2, :], src[HALF:P, :], ACT.Copy)
                nc.scalar.activation(swap[HALF:P, a % 2, :], src[0:HALF, :], ACT.Copy).then_inc(swapped, 1)

            def kq_hi(g, bp, c):
                act.wait_ge(rope_done, cnt(5, g, bp, c + 1))
                if c:
                    nc.scalar.activation(qh[:, c - 1], second(q[:, c - 1]), ACT.Copy).then_inc(kqh_done, 1)
                else:
                    wait(act, scores_ps, cnt(8, g, bp, -8))
                    nc.scalar.activation(kh[:, bp, :], k[:, bp, :], ACT.Copy).then_inc(kqh_done, 1)

            def v_out(g, bp):
                act.wait_ge(proj_ps, cnt(6, g, bp, 2))
                wait(act, v_ps, cnt(1, g, bp, 0))
                nc.scalar.activation(vT[:, :], PJ_B[1][:, :], ACT.Copy).then_inc(vT_done, 1)

            def v_hi(g, bp, t_bank):
                act.wait_ge(v_ps, cnt(1, g, bp, 1))
                wait(act, o_ps, cnt(4, g, bp, -4))
                nc.scalar.activation(vh[:, bp].rearrange("p t n -> p (t n)"), t_bank[:, :],
                                     ACT.Copy).then_inc(vh_done, 1)

            def exps(g, bp, b, h):
                s = 4 * b + h
                act.wait_ge(nmax_done, cnt(8, g, bp, s + 1))
                for i, (c0, c1) in enumerate(((0, P), (P, 3 * P))):
                    e = nc.scalar.activation(probs[:, s, c0:c1], probs[:, s, c0:c1], ACT.Exp,
                                             bias=nmx[:, s, i:i + 1], scale=SM, accum_out=rsum[:, s, i:i + 1])
                e.then_inc(exp_done, 1)

            def p_hi(g, bp, b, r):
                j = 4 * b + r
                act.wait_ge(pT_ps, cnt(6, g, bp, 3 * b + r + 1))
                wait(act, o_ps, cnt(4, g, bp, 2 * b))
                nc.scalar.activation(ph[:, r, :], T_B[(7 * bp + j) % 2][:, :], ACT.Copy).then_inc(ph_done, 1)

            def o_hi(g, bp, j):
                act.wait_ge(o_ps, cnt(4, g, bp, j + 1))
                wait(act, y_ps, cnt(4, g, bp, j - 3))
                nc.scalar.activation(oh[:, j].rearrange("p h n -> p (h n)"), O_B[j % 2][:, :],
                                     ACT.Copy).then_inc(oh_done, 1)

            act.wait_ge(ab_ps, 4 * FT)
            for c in range(6):
                hi_in(0, c)
            hid_hi(10, 5, 0, 0)
            hid_hi(10, 5, 0, 1)
            halves(0, 0, 0)
            v_out(0, 0)
            for t in range(NT):
                act.wait_ge(ffn_read, 5 * NT + t + 1)
                nc.scalar.activation(gate[:, t, :], gate[:, t, :], ACT.Silu).then_inc(gate_done, 1)
            halves(0, 0, 1)
            v_hi(0, 0, T_B[1])
            kq_hi(0, 0, 0)
            for c in range(2, 5):
                halves(0, 0, c)
                kq_hi(0, 0, c - 1)
            kq_hi(0, 0, 4)
            for h in range(GH):
                exps(0, 0, 0, h)

            def step(g, bp, last):
                ng, nbp = (g, 1) if bp == 0 else (g + 1, 0)
                w = bp == 0
                nxt = w and not last
                if last and bp == 1:
                    p_hi(g, bp, 0, 0)
                    p_hi(g, bp, 0, 1)
                    exps(g, bp, 1, 2)
                    exps(g, bp, 1, 3)
                    p_hi(g, bp, 0, 2)
                    o_hi(g, bp, 0)
                    o_hi(g, bp, 1)
                    for r in range(3):
                        p_hi(g, bp, 1, r)
                    o_hi(g, bp, 2)
                    o_hi(g, bp, 3)
                    return
                for r in range(3):
                    p_hi(g, bp, 0, r)
                halves(ng, nbp, 0)
                v_out(ng, nbp)
                if w:
                    hi_wo(g, 0)
                    hi_wo(g, 1)
                o_hi(g, bp, 0)
                o_hi(g, bp, 1)
                if w:
                    hi_wo(g, 2)
                    hi_wo(g, 3)
                exps(g, bp, 1, 0)
                halves(ng, nbp, 1)
                exps(g, bp, 1, 1)
                exps(g, bp, 1, 2)
                exps(g, bp, 1, 3)
                v_hi(ng, nbp, T_B[(7 * bp + 3) % 2])
                halves(ng, nbp, 2)
                kq_hi(ng, nbp, 0)
                p_hi(g, bp, 1, 0)
                halves(ng, nbp, 3)
                p_hi(g, bp, 1, 1)
                kq_hi(ng, nbp, 1)
                p_hi(g, bp, 1, 2)
                kq_hi(ng, nbp, 2)
                halves(ng, nbp, 4)
                kq_hi(ng, nbp, 3)
                o_hi(g, bp, 2)
                o_hi(g, bp, 3)
                kq_hi(ng, nbp, 4)
                for h in range(GH):
                    exps(ng, nbp, 0, h)
                if last:
                    exps(ng, nbp, 1, 0)
                    exps(ng, nbp, 1, 1)
                if nxt:
                    for c in range(6):
                        hi_in(g + 1, c)

            def group(g, last=False):
                step(g, 0, last)
                step(g, 1, last)

            group(0)
            with act.Fori(1, NKV - 1) as g:
                group(g)
            group(NKV - 1, True)

        @block.vector
        def _(dve):
            def small(i, part, fn, *args):
                dve.wait_ge(ln_small, 6 * part + i)
                fn(*args).then_inc(ln_small, 1)

            def statistics(part):
                tiles = range(4 * part, 4 * part + 4)
                for i in tiles:
                    dve.wait_ge(x_in[i], 16)
                    nc.vector.bn_stats(stat[:, i, :], xn[:, i, :]).then_inc(stats_done, 1)
                for i in tiles:
                    dve.wait_ge(stats_done, i + 1)
                    nc.vector.bn_aggr(mv[:, i, :], stat[:, i, :]).then_inc(mv_done, 1)
                dve.wait_ge(mv_done, tiles[-1] + 1)
                v, r0, r, t = [std[:, n, 4 * part:4 * part + 4] for n in (0, 1, 2, 3)]
                nc.vector.tensor_scalar(v, mv[:, tiles[0]:tiles[-1] + 1, 1], EPS, None, ALU.add) \
                    .then_inc(ln_small, 1)
                dve.wait_ge(std_done, part + 1)
                nc.vector.reciprocal(r, r0).then_inc(ln_small, 1)
                small(2, part, nc.vector.tensor_tensor, t, r, r, ALU.mult)
                small(3, part, nc.vector.tensor_tensor, r0, t, v, ALU.mult)
                small(4, part, nc.vector.tensor_scalar, t, r0, -0.5, 1.5, ALU.mult, ALU.add)
                small(5, part, nc.vector.tensor_tensor, r0, t, r, ALU.mult)
                dve.wait_ge(ln_small, 6 * part + 6)

            def norm(i):
                nc.vector.tensor_scalar(xn[:, i, :], xn[:, i, :], mv[:, i, 0:1], std[:, 1, i:i + 1],
                                        ALU.subtract, ALU.mult).then_inc(xn_done, 1)

            def x_lo(i):
                dve.wait_ge(xh_done, i + 1)
                cols = slice(i * P, (i + 1) * P)
                nc.vector.tensor_tensor(xl[:, :, cols], bank[X_B[i]][:, :].rearrange("p (t n) -> p t n", t=DT),
                                        xh[:, :, cols].bitcast(f32), ALU.subtract).then_inc(xl_done, 1)

            def dequant13(t, s, use):
                dve.wait_ge(w13_in[s], 32 * use)
                wait(dve, W13_done, t)
                src = packed[:, s].rearrange("p m c -> p (m c)")
                nc.vector.tensor_scalar(nib[:, 0, :], src, 4, None, ALU.arith_shift_right)
                nc.vector.tensor_scalar(nib[:, 1, :], src, 15, 8, ALU.bitwise_and, ALU.bitwise_xor) \
                    .then_inc(nib_done, 1)
                dve.wait_ge(nib_done, t + 1)
                wait(dve, W13_ps, 2 * t - 2)
                n = [nib[:, i, :].rearrange("p (g c) -> p g c", c=GROUP) for i in range(2)]
                sc = s13[:, bass.ds(t, 1), :, :].rearrange("p o m (g n) -> p n (o m g)", n=2)
                o = W13[:, s].rearrange("p m (g n c) -> p n (m g) c", n=2, c=GROUP)
                GS = 2 * DT
                nc.vector.tensor_tensor(o[:, 0], n[0], spread(sc[:, 0].unsqueeze(2), P, GS, GROUP), ALU.mult)
                nc.vector.scalar_tensor_tensor(out=o[:, 1], in0=n[1], scalar=-8.0,
                                               in1=spread(sc[:, 1].unsqueeze(2), P, GS, GROUP),
                                               op0=ALU.add, op1=ALU.mult).then_inc(W13_done, 1)

            def w13_lo(t, s2_):
                for m in range(2):
                    dve.wait_ge(W13h_done, 2 * t + (m + 1))
                    nc.vector.tensor_tensor(W13l[:, s2_, m].rearrange("p t n -> p (t n)"), bank[m][:, :],
                                            W13h[:, s2_, m].rearrange("p t n -> p (t n)").bitcast(f32),
                                            ALU.subtract).then_inc(W13l_done, 1)

            def hid(t, half):
                dve.wait_ge(silu_done, 2 * t + (half + 1))
                dve.wait_ge(ab_ps, 4 * t + (2 * half + 2))
                nc.vector.tensor_tensor(act_h[:, half, :], act_h[:, half, :], bank[3 + 2 * half][:, :],
                                        ALU.mult).then_inc(h_done, 1)

            def dequant2(i):
                r0, r1 = NR2 * i, min(NR2 * i + NR2, R2)
                n = r1 - r0
                dve.wait_ge(w2_in[i % 2], 16 * (i // 2 + 1))
                wait(dve, W2_done, i)
                src = packed2[:, i % 2, 0:n * GROUP]
                nc.vector.tensor_scalar(nib2[:, 0, 0:n * GROUP], src, 4, None, ALU.arith_shift_right)
                nc.vector.tensor_scalar(nib2[:, 1, 0:n * GROUP], src, 15, 8, ALU.bitwise_and,
                                        ALU.bitwise_xor).then_inc(nib2_done, 1)
                dve.wait_ge(nib2_done, i + 1)
                nb = [nib2[:, a, 0:n * GROUP].rearrange("p (r c) -> p r c", c=GROUP) for a in range(2)]
                sc = s2s[:, 2 * r0:2 * r1].rearrange("p (r n) -> p n r", n=2)
                nc.vector.tensor_tensor(W2n[:, r0:r1, 0, :], nb[0], spread(sc[:, 0].unsqueeze(2), P, n, GROUP),
                                        ALU.mult)
                nc.vector.scalar_tensor_tensor(out=W2n[:, r0:r1, 1, :], in0=nb[1], scalar=-8.0,
                                               in1=spread(sc[:, 1].unsqueeze(2), P, n, GROUP),
                                               op0=ALU.add, op1=ALU.mult).then_inc(W2_done, 1)

            def ffn_add(u):
                for i in range(NT):
                    dve.wait_ge(ffn_ps, 8 * u + (i + 1))
                    src = bank[7 - i % 2][:, :]
                    if isinstance(u, int) and u == 0:
                        nc.vector.tensor_copy(gate[:, i, :], src).then_inc(ffn_read, 1)
                    else:
                        dve.wait_ge(ffn_read, 8 * u + (i - 7))
                        nc.vector.tensor_tensor(gate[:, i, :], gate[:, i, :], src, ALU.add).then_inc(ffn_read, 1)

            statistics(0)
            dve.wait_ge(zeroed, 1)
            for i in range(4):
                norm(i)
            dve.wait_ge(s13_in, 64)
            dequant13(0, 0, 1)
            for i in range(4):
                x_lo(i)
            w13_lo(0, 0)
            statistics(1)
            for i in range(4, NT):
                norm(i)
            dequant13(1, 1, 1)
            for i in range(4, NT):
                x_lo(i)
            hid(0, 0)
            dve.wait_ge(s2_in, 16)
            dequant2(0)
            w13_lo(1, 1)
            hid(0, 1)
            dequant2(1)
            dequant13(2, 0, 2)
            hid(1, 0)
            dequant2(2)
            w13_lo(2, 0)
            dequant2(3)
            hid(1, 1)
            dequant13(3, 1, 2)
            hid(2, 0)
            w13_lo(3, 1)
            hid(2, 1)
            dequant13(4, 0, 3)
            ffn_add(0)

            def two_tiles(v):
                hid(2 * v + 3, 0)
                w13_lo(2 * v + 4, 0)
                hid(2 * v + 3, 1)
                dequant13(2 * v + 5, 1, v + 3)
                hid(2 * v + 4, 0)
                ffn_add(v + 1)
                w13_lo(2 * v + 5, 1)
                hid(2 * v + 4, 1)
                dequant13(2 * v + 6, 0, v + 4)

            two_tiles(0)
            with dve.Fori(1, 3) as v:
                two_tiles(v)
            hid(9, 0)
            w13_lo(10, 0)
            hid(9, 1)
            hid(10, 0)
            hid(10, 1)
            ffn_add(4)

            def cos_part(g, bp, c):
                dve.wait_ge(swapped, cnt(5, g, bp, c + 1))
                if c == 0:
                    wait(dve, scores_ps, cnt(8, g, bp, -8))
                dst = q[:, c - 1, :] if c else k[:, bp, :]
                nc.vector.tensor_tensor(dst.rearrange("p (b n) -> p b n", b=2),
                                        PJ_B[(c + 1 if c else 0) % 2][:, :].rearrange("p (b n) -> p b n", b=2),
                                        spread(cos.unsqueeze(1), P, 2, SEQ), ALU.mult).then_inc(cos_done, 1)

            def rotate(g, bp, c):
                dve.wait_ge(sin_done, cnt(5, g, bp, c + 1))
                dve.wait_ge(cos_done, cnt(5, g, bp, c + 1))
                dst = q[:, c - 1, :] if c else k[:, bp, :]
                nc.vector.tensor_tensor(dst, dst, swap[:, (5 * bp + c) % 2, :], ALU.add).then_inc(rope_done, 1)

            def kq_lo(g, bp, c):
                dve.wait_ge(kqh_done, cnt(5, g, bp, c + 1))
                if c:
                    nc.vector.tensor_tensor(ql[:, c - 1], second(q[:, c - 1]), qh[:, c - 1].bitcast(f32),
                                            ALU.subtract).then_inc(kql_done, 1)
                else:
                    nc.vector.tensor_tensor(kl[:, bp, :], k[:, bp, :], kh[:, bp, :].bitcast(f32),
                                            ALU.subtract).then_inc(kql_done, 1)

            def negate(g, bp, b, h):
                s = 4 * b + h
                dve.wait_ge(masked, cnt(8, g, bp, s + 1))
                nc.vector.tensor_scalar(nmx[:, s, :], mx[:, s, :], -SM, None, ALU.mult).then_inc(nmax_done, 1)

            def masking(g, bp, b, h0):
                wait(dve, pT_ps, cnt(6, g, bp, 3 * b - 3))
                for h in (h0, h0 + 1):
                    s = 4 * b + h
                    dve.wait_ge(scores_ps, cnt(8, g, bp, s + 1))
                    if h > h0:
                        negate(g, bp, b, h0)
                    else:
                        nc.vector.memset(pace[:, s // 2:s // 2 + 1], 0.0)
                    for i, (c0, c1) in enumerate(((0, P), (P, 3 * P))):
                        m = nc.vector.tensor_tensor_reduce(
                            out=probs[:, s, c0:c1], in0=S_B[s % 2][:, c0:c1], in1=mask[:, c0:c1], scale=1.0,
                            scalar=NEG, op0=ALU.add, op1=ALU.max, accum_out=mx[:, s, i:i + 1])
                    m.then_inc(masked, 1)
                negate(g, bp, b, h0 + 1)

            def normalise(g, bp, b, h):
                s = 4 * b + h
                dve.wait_ge(exp_done, cnt(8, g, bp, s + 1))
                nc.vector.reciprocal(rinv[:, s, :], rsum[:, s, :]).then_inc(rinv_done, 1)
                dve.wait_ge(rinv_done, cnt(8, g, bp, s + 1))
                for i, (c0, c1) in enumerate(((0, P), (P, 3 * P))):
                    m = nc.vector.tensor_scalar(probs[:, s, c0:c1], probs[:, s, c0:c1], rinv[:, s, i:i + 1], None,
                                                ALU.mult)
                m.then_inc(probs_done, 1)

            def p_lo(g, bp, b, r):
                dve.wait_ge(ph_done, cnt(6, g, bp, 3 * b + r + 1))
                nc.vector.tensor_tensor(pl[:, r, :], T_B[(7 * bp + 4 * b + r) % 2][:, :], ph[:, r, :].bitcast(f32),
                                        ALU.subtract).then_inc(pl_done, 1)

            def v_lo(g, bp, t_bank):
                dve.wait_ge(vh_done, cnt(1, g, bp, 1))
                nc.vector.tensor_tensor(vl[:, bp].rearrange("p t n -> p (t n)"), t_bank[:, :],
                                        vh[:, bp].rearrange("p t n -> p (t n)").bitcast(f32),
                                        ALU.subtract).then_inc(vl_done, 1)

            def o_lo(g, bp, j):
                dve.wait_ge(oh_done, cnt(4, g, bp, j + 1))
                nc.vector.tensor_tensor(ol[:, j].rearrange("p h n -> p (h n)"), O_B[j % 2][:, :],
                                        oh[:, j].rearrange("p h n -> p (h n)").bitcast(f32),
                                        ALU.subtract).then_inc(ol_done, 1)

            def accumulate(g, bp, t):
                dve.wait_ge(y_ps, cnt(4, g, bp, t + 1))
                wait(dve, acc_done, cnt(4, g, bp, t - 7))
                a, o = acc[:, 4 * bp + t, :], O_B[t % 2][:, :]
                if isinstance(g, int) and g == 0:
                    nc.vector.tensor_copy(a, o).then_inc(acc_done, 1)
                else:
                    nc.vector.tensor_tensor(a, a, o, ALU.add).then_inc(acc_done, 1)

            def finish(bp, t):
                n = 4 * bp + t
                dve.wait_ge(y_ps, cnt(4, NKV - 1, bp, t + 1))
                dve.wait_ge(rest_done, n + 1)
                nc.vector.tensor_tensor(gate[:, n, :], O_B[t % 2][:, :], gate[:, n, :], ALU.mult).then_inc(acc_done, 1)
                if n == NT - 1:
                    dve.wait_ge(acc_done, ALL_Y)
                    nc.vector.tensor_tensor(gate[:, n, :], gate[:, n, :], acc[:, n, :], ALU.add) \
                        .then_inc(last_final, 1)

            dve.wait_ge(hl_done, 2 * FT)
            cos_part(0, 0, 0)
            ffn_add(FT // 2)
            rotate(0, 0, 0)
            cos_part(0, 0, 1)
            v_lo(0, 0, T_B[1])
            rotate(0, 0, 1)
            kq_lo(0, 0, 0)
            for c in range(2, 5):
                cos_part(0, 0, c)
                rotate(0, 0, c)
                kq_lo(0, 0, c - 1)
            kq_lo(0, 0, 4)
            dve.wait_ge(const_in, 16)
            masking(0, 0, 0, 0)
            masking(0, 0, 0, 2)
            for h in range(GH):
                normalise(0, 0, 0, h)

            def step(g, bp, last):
                ng, nbp = (g, 1) if bp == 0 else (g + 1, 0)
                if last and bp == 1:
                    p_lo(g, bp, 0, 0)
                    p_lo(g, bp, 0, 1)
                    normalise(g, bp, 1, 0)
                    finish(0, 2)
                    normalise(g, bp, 1, 1)
                    finish(0, 3)
                    p_lo(g, bp, 0, 2)
                    normalise(g, bp, 1, 2)
                    normalise(g, bp, 1, 3)
                    o_lo(g, bp, 0)
                    o_lo(g, bp, 1)
                    p_lo(g, bp, 1, 0)
                    p_lo(g, bp, 1, 1)
                    finish(1, 0)
                    p_lo(g, bp, 1, 2)
                    finish(1, 1)
                    o_lo(g, bp, 2)
                    o_lo(g, bp, 3)
                    finish(1, 2)
                    finish(1, 3)
                    return
                for r in range(3):
                    p_lo(g, bp, 0, r)
                cos_part(ng, nbp, 0)
                o_lo(g, bp, 0)
                o_lo(g, bp, 1)
                rotate(ng, nbp, 0)
                masking(g, bp, 1, 0)
                normalise(g, bp, 1, 0)
                masking(g, bp, 1, 2)
                cos_part(ng, nbp, 1)
                normalise(g, bp, 1, 1)
                normalise(g, bp, 1, 2)
                normalise(g, bp, 1, 3)
                v_lo(ng, nbp, T_B[(7 * bp + 3) % 2])
                rotate(ng, nbp, 1)
                cos_part(ng, nbp, 2)
                kq_lo(ng, nbp, 0)
                p_lo(g, bp, 1, 0)
                rotate(ng, nbp, 2)
                cos_part(ng, nbp, 3)
                p_lo(g, bp, 1, 1)
                kq_lo(ng, nbp, 1)
                p_lo(g, bp, 1, 2)
                kq_lo(ng, nbp, 2)
                rotate(ng, nbp, 3)
                cos_part(ng, nbp, 4)
                o_lo(g, bp, 2)
                kq_lo(ng, nbp, 3)
                o_lo(g, bp, 3)
                rotate(ng, nbp, 4)
                masking(ng, nbp, 0, 0)
                kq_lo(ng, nbp, 4)
                if last:
                    finish(0, 0)
                    masking(ng, nbp, 0, 2)
                    normalise(ng, nbp, 0, 0)
                    normalise(ng, nbp, 0, 1)
                    masking(ng, nbp, 1, 0)
                    normalise(ng, nbp, 0, 2)
                    normalise(ng, nbp, 0, 3)
                    finish(0, 1)
                    masking(ng, nbp, 1, 2)
                    return
                accumulate(g, bp, 0)
                masking(ng, nbp, 0, 2)
                normalise(ng, nbp, 0, 0)
                normalise(ng, nbp, 0, 1)
                accumulate(g, bp, 1)
                normalise(ng, nbp, 0, 2)
                normalise(ng, nbp, 0, 3)
                accumulate(g, bp, 2)
                accumulate(g, bp, 3)

            def group(g, last=False):
                step(g, 0, last)
                step(g, 1, last)

            group(0)
            with dve.Fori(1, NKV - 1) as g:
                group(g)
            group(NKV - 1, True)

        @block.tensor
        def _(pe):
            def three(out_, pairs, ahead=None):
                n = len(pairs)
                for i, (sh, sl, mh, ml) in enumerate(pairs):
                    if ahead and i in ahead:
                        ahead[i]()
                    nc.tensor.matmul(out_, sh, mh, start=(i == 0), stop=False)
                    nc.tensor.matmul(out_, sh, ml, start=False, stop=False)
                    m = nc.tensor.matmul(out_, sl, mh, start=False, stop=(i == n - 1))
                return m

            pe.wait_ge(const_in, 16)
            def x_turn(tiles):
                for i in tiles:
                    pe.wait_ge(xn_done, i + 1)
                    for d in range(DT):
                        m = nc.tensor.transpose(bank[X_B[i]][:, d * P:(d + 1) * P], xn[:, i, d * P:(d + 1) * P], ident)
                    m.then_inc(xT_ps, 1)

            def w13_turn(t, s2_):
                pe.wait_ge(W13_done, t + 1)
                for m in range(2):
                    wait(pe, W13l_done, 2 * t + (m - 1))
                    for d in range(DT):
                        i = nc.tensor.transpose(bank[m][:, d * P:(d + 1) * P],
                                                W13[:, s2_, m, d * P:(d + 1) * P], ident)
                    i.then_inc(W13_ps, 1)

            def w13_mult(t, s, between=None):
                between = between or {}
                for half in range(2):
                    wait(pe, h_done, 2 * t + (half - 1))
                    if isinstance(t, int) and t == 0:
                        pe.wait_ge(xl_done, 4 * (half + 1))
                    cols = slice(half * IT, half * IT + IT)
                    for m in range(2):
                        pe.wait_ge(W13l_done, 2 * t + (m + 1))
                        three(bank[2 + 2 * half + m][:, :],
                              [(W13h[:, s, m, d, :], W13l[:, s, m, d, :], xh[:, d, cols], xl[:, d, cols])
                               for d in range(DT)]).then_inc(ab_ps, 1)
                        for act_ in between.get(2 * half + m, ()):
                            act_()

            def w2_turn(t):
                rows = P if t < FT - 1 else FR
                pe.wait_ge(W2_done, 4)
                wait(pe, W2h_done, t - 1)
                W2f = W2n[:, :, :, :].rearrange("p r n c -> p (r n c)")
                for j in range(4):
                    i = nc.tensor.transpose(bank[6 + t % 2][0:rows, j * P:(j + 1) * P],
                                            W2f[:, j * F + t * P:j * F + t * P + rows], ident)
                i.then_inc(W2_ps, 1)

            def w2_mult(u, pair):
                if isinstance(u, int):
                    pe.wait_ge(W2l_done, min(2 * u + 2, FT))
                pe.wait_ge(hl_done, 4 * u + 2 * len(pair))
                for i in range(NT):
                    if isinstance(u, int) and u == 0 and i < 2:
                        pe.wait_ge(W2h_done, FT - 1 + i)
                    else:
                        pe.wait_ge(ffn_read, 8 * u + (i - 1))
                    cols = slice(i * P, (i + 1) * P)
                    three(bank[7 - i % 2][:, :],
                          [(hh[:, s, cols], hl[:, s, cols],
                            W2h[:, bass.ds(2 * u + e, 1), :].rearrange("p o d -> p (o d)"),
                            W2l[:, bass.ds(2 * u + e, 1), :].rearrange("p o d -> p (o d)"))
                           for e, s in enumerate(pair)]).then_inc(ffn_ps, 1)

            def turns2(*tiles):
                return [lambda t=t: w2_turn(t) for t in tiles]

            x_turn(range(4))
            w13_turn(0, 0)
            w13_mult(0, 0, {0: [lambda: x_turn(range(4, NT))], 2: [lambda: w13_turn(1, 1)]})
            w13_mult(1, 1, {2: [lambda: w13_turn(2, 0)]})
            w13_mult(2, 0, {0: turns2(0, 1), 1: turns2(2, 3), 2: turns2(4, 5) + [lambda: w13_turn(3, 1)],
                            3: turns2(6, 7)})
            w13_mult(3, 1, {0: turns2(8, 9), 1: turns2(10) + [lambda: w2_mult(0, (0, 1))],
                            2: [lambda: w13_turn(4, 0)]})
            w13_mult(4, 0, {1: [lambda: w2_mult(1, (0, 1))], 2: [lambda: w13_turn(5, 1)]})
            pe.wait_ge(W2l_done, FT)
            with pe.Fori(1, 3) as v:
                w13_mult(2 * v + 3, 1, {2: [lambda: w13_turn(2 * v + 4, 0)]})
                w13_mult(2 * v + 4, 0, {1: [lambda: w2_mult(v + 1, (0, 1))], 2: [lambda: w13_turn(2 * v + 5, 1)]})
            w13_mult(9, 1, {2: [lambda: w13_turn(10, 0)]})
            w13_mult(10, 0)
            w2_mult(4, (0, 1))

            def project(g, bp, c, ahead=None):
                if bp == 0:
                    pe.wait_ge(wl_done, in_chunk(g, c) + 1)
                if c == 3:
                    wait(pe, vT_done, cnt(1, g, bp, 1))
                else:
                    r = {0: -1, 1: 0, 2: 1, 4: 2, 5: 3}[c]
                    wait(pe, cos_done, cnt(5, g, bp, r))
                cols = slice(bp * IT, bp * IT + IT)
                three(PJ_B[c % 2][:, :],
                      [(wih[:, c, d, :], wil[:, c, d, :], xh[:, d, cols], xl[:, d, cols])
                       for d in range(DT)], ahead).then_inc(proj_ps, 1)

            def v_turn(g, bp, t_bank):
                pe.wait_ge(vT_done, cnt(1, g, bp, 1))
                for t in range(IT // P):
                    i = nc.tensor.transpose(t_bank[:, t * P:(t + 1) * P], vT[:, t * P:(t + 1) * P], ident)
                i.then_inc(v_ps, 1)

            def scores(g, bp, b, h):
                s = 4 * b + h
                if b == 0:
                    pe.wait_ge(rope_done, cnt(5, g, bp, h + 2))
                wait(pe, masked, cnt(8, g, bp, s - 1))
                c = b * SEQ
                nc.tensor.matmul(S_B[s % 2][:, 0:P], q[:, h, c:c + P], k[:, bp, c:c + P], start=True, stop=True)
                if b == 0:
                    pe.wait_ge(kql_done, cnt(5, g, bp, h + 2))
                three(S_B[s % 2][:, P:3 * P], [(qh[:, h, b, :], ql[:, h, b, :], kh[:, bp, c:c + SEQ],
                                                kl[:, bp, c:c + SEQ])]).then_inc(scores_ps, 1)

            def p_turn(g, bp, b, r, last=False):
                j = 4 * b + r
                if r == 0:
                    pe.wait_ge(probs_done, cnt(8, g, bp, 4 * b + 4))
                if j == 5:
                    if last:
                        pe.wait_ge(pl_done, cnt(6, g, bp, 2))
                    else:
                        pe.wait_ge(vl_done, cnt(1, g, bp, 2))
                else:
                    wait(pe, pl_done, cnt(6, g, bp, {0: -1, 1: 0, 2: 1, 4: 3, 6: 4}[j]))
                    if j == 1:
                        pe.wait_ge(vl_done, cnt(1, g, bp, 1))
                for h in range(GH):
                    i = nc.tensor.transpose(T_B[(7 * bp + j) % 2][:, h * P:(h + 1) * P],
                                            probs[:, 4 * b + h, r * P:(r + 1) * P], ident)
                i.then_inc(pT_ps, 1)

            def attend(g, bp, b, late=False):
                pe.wait_ge(vl_done, cnt(1, g, bp, 1))
                for t in range(2):
                    j = 2 * b + t
                    if b == 0:
                        wait(pe, acc_done, cnt(4, g, bp, t - 1))
                    else:
                        pe.wait_ge(ol_done, cnt(4, g, bp, t + 1))
                    if late:
                        pe.wait_ge(acc_done, cnt(4, g, bp, t + 1))
                    blocks = ((0, 0),) if t == 0 else ((1, 0), (2, 1))
                    pe.wait_ge(pl_done, cnt(6, g, bp, 3 * b + (1 if t == 0 else 3)))
                    three(O_B[j % 2][:, :], [(vh[:, bp, 2 * b + kt, :], vl[:, bp, 2 * b + kt, :],
                                              ph[:, r, :], pl[:, r, :]) for r, kt in blocks]).then_inc(o_ps, 1)

            def out_project(g, bp, t, early=False):
                pe.wait_ge(ol_done, cnt(4, g, bp, t + 1 if t > 1 or early else t + 3))
                if t > 1:
                    pe.wait_ge(acc_done, cnt(4, g, bp, t - 1))
                if bp == 0 and t == 0:
                    pe.wait_ge(wl_done, wo_chunk(g, GH - 1) + 1)
                three(O_B[t % 2][:, :], [(oh[:, t, h, :], ol[:, t, h, :], woh[:, h, :], wol[:, h, :])
                                         for h in range(GH)]).then_inc(y_ps, 1)

            pe.wait_ge(h_done, 2 * FT)
            project(0, 0, 0)
            project(0, 0, 1)
            w2_mult(FT // 2, (0,))
            project(0, 0, 2)
            v_turn(0, 0, T_B[1])
            for c in range(3, 6):
                project(0, 0, c)
            scores(0, 0, 0, 0)
            scores(0, 0, 0, 1)
            project(0, 1, 0)
            scores(0, 0, 0, 2)
            scores(0, 0, 0, 3)
            project(0, 1, 1)

            def step(g, bp, last):
                begun = isinstance(g, int) and g == 0 and bp == 0
                ng, nbp = (g, 1) if bp == 0 else (g + 1, 0)
                if last and bp == 1:
                    p_turn(g, bp, 0, 0, True)
                    p_turn(g, bp, 0, 1, True)
                    out_project(g, 0, 3)
                    p_turn(g, bp, 0, 2, True)
                    attend(g, bp, 0)
                    p_turn(g, bp, 1, 0, True)
                    p_turn(g, bp, 1, 1, True)
                    out_project(g, bp, 0, True)
                    p_turn(g, bp, 1, 2, True)
                    out_project(g, bp, 1, True)
                    attend(g, bp, 1, True)
                    out_project(g, bp, 2)
                    out_project(g, bp, 3)
                    return
                p_turn(g, bp, 0, 0)
                p_turn(g, bp, 0, 1)
                if not begun:
                    project(ng, nbp, 0)
                p_turn(g, bp, 0, 2)
                if not begun:
                    project(ng, nbp, 1)
                attend(g, bp, 0)
                scores(g, bp, 1, 0)
                scores(g, bp, 1, 1)
                project(ng, nbp, 2)
                scores(g, bp, 1, 2)
                scores(g, bp, 1, 3)
                pe.wait_ge(pl_done, cnt(6, g, bp, 2))
                v_turn(ng, nbp, T_B[(7 * bp + 3) % 2])
                project(ng, nbp, 3)
                project(ng, nbp, 4, {3: lambda: p_turn(g, bp, 1, 0)})
                p_turn(g, bp, 1, 1)
                project(ng, nbp, 5, {2: lambda: p_turn(g, bp, 1, 2)})
                attend(g, bp, 1)
                scores(ng, nbp, 0, 0)
                scores(ng, nbp, 0, 1)
                out_project(g, bp, 0)
                scores(ng, nbp, 0, 2)
                scores(ng, nbp, 0, 3)
                if last:
                    out_project(g, bp, 1)
                    scores(ng, nbp, 1, 0)
                    scores(ng, nbp, 1, 1)
                    out_project(g, bp, 2)
                    scores(ng, nbp, 1, 2)
                    scores(ng, nbp, 1, 3)
                    return
                out_project(g, bp, 1)
                out_project(g, bp, 2)
                out_project(g, bp, 3)

            def group(g, last=False):
                step(g, 0, last)
                step(g, 1, last)

            group(0)
            with pe.Fori(1, NKV - 1) as g:
                group(g)
            group(NKV - 1, True)


def constants():
    inv = (np.float32(10000.0) ** (-np.arange(HALF, dtype=np.float32) / np.float32(HALF))).astype(np.float32)
    ang = np.arange(SEQ, dtype=np.float32)[None, :] * inv[:, None]
    cos, sin = np.cos(ang), np.sin(ang)
    c = np.zeros((P, C_W), np.float32)
    c[:, C_COS:C_COS + SEQ] = np.concatenate([cos, cos])
    c[:, C_SIN:C_SIN + SEQ] = np.concatenate([-sin, sin])
    i, j = np.arange(P)[:, None], np.arange(P)[None, :]
    for n, ok in enumerate((j <= i, j > i, j <= i)):
        c[:, C_MASK + n * P:C_MASK + (n + 1) * P] = np.where(ok, 0.0, NEG)
    c[:, C_ID:C_ID + P] = np.eye(P)
    return c


_INS = ["L0_attn_x", "L0_attn_wq", "L0_attn_wk", "L0_attn_wv", "L0_attn_wo",
        "L0_ffn_w1", "L0_ffn_s1", "L0_ffn_w2", "L0_ffn_s2", "L0_ffn_w3", "L0_ffn_s3"]


def kernel(**inputs):
    import numpy as _np
    import concourse.bacc as _bacc
    from concourse import mybir as _mybir
    from concourse.bass_utils import run_bass_kernel_spmd as _run

    nc = _bacc.Bacc("TRN2", target_bir_lowering=False, num_devices=1)
    arrays, args = {}, []
    for name, a in [(n, inputs[n]) for n in _INS] + [("constants", constants())]:
        a = _np.ascontiguousarray(a)
        arrays[f"in_{name}"] = a
        args.append(nc.dram_tensor(f"in_{name}", a.shape, _mybir.dt.from_np(a.dtype), kind="ExternalInput").ap())
    args.append(nc.dram_tensor("out_0", (B, SEQ, D), _mybir.dt.float32, kind="ExternalOutput").ap())
    build(nc, *args)
    r = _run(nc, [arrays], core_ids=[0])
    return r.results[0]["out_0"]
```
